# Optimizing a Trainium2 kernel written in Bass

```python
import numpy as np
import jax
import jax.numpy as jnp

def _softmax(x, axis=-1):
    return jax.nn.softmax(x, axis=axis)

def _gelu(x):
    return jax.nn.gelu(x, approximate=True)

def _silu(x):
    return jax.nn.silu(x)

def _sigmoid(x):
    return jax.nn.sigmoid(x)

def _layernorm(x, axis=-1, eps=1e-05):
    m = jnp.mean(x, axis=axis, keepdims=True)
    v = jnp.var(x, axis=axis, keepdims=True)
    return (x - m) / jnp.sqrt(v + eps)

def _scatter_add(tgt, idx, src, axis=0):
    return tgt.at[idx].add(src)

def _segment_sum(src, seg, n):
    return jax.ops.segment_sum(src, seg, n)
kernel_name = 'mk_gnn_ffn_d1_gnn_r64_27c195'

def setup_inputs(seed: int=0):
    np.random.seed(seed)
    _w = jnp.asarray

    def _rec_inputs():
        import jax
        import jax.numpy as jnp
        _gk = jax.random.key(seed)
        x = -0.0003713 + 1 * jax.random.normal(jax.random.fold_in(_gk, 1), (50000, 256), jnp.float32)
        src = jax.random.randint(jax.random.fold_in(_gk, 2), (25000,), 0, 50000, jnp.int32)
        dst = jax.random.randint(jax.random.fold_in(_gk, 3), (25000,), 0, 50000, jnp.int32)
        _o = jnp.argsort(dst, stable=True)
        src = src[_o]
        dst = dst[_o]
        edge_weight = 0.00107675 + 0.999702 * jax.random.normal(jax.random.fold_in(_gk, 12), (25000,), jnp.float32)
        return (x, src, dst, edge_weight)
    x, src, dst, edge_weight = _rec_inputs()

    def _L0_gnn_setup():
        import jax, jax.numpy as jnp
        import numpy as np
        N = 50000
        NNZ = 12500
        D = 256
        key = jax.random.key(seed)
        k1, k2, k3, k4 = jax.random.split(key, 4)
        m = jax.random.normal(k1, (N, D), dtype=jnp.float32)
        row = jnp.sort(jax.random.randint(k2, (NNZ,), 0, N))
        col = jax.random.randint(k3, (NNZ,), 0, N)
        vals = jax.random.normal(k4, (NNZ,), dtype=jnp.float32)
        return {'m': m, 'row': row, 'col': col, 'vals': vals}
    _L0_gnn_all = _L0_gnn_setup()
    _L0_gnn_in = {k: v for k, v in _L0_gnn_all.items() if k in ()}
    del _L0_gnn_all

    def _L0_ffn_setup():
        import math
        import jax, jax.numpy as jnp
        import numpy as np
        CAPACITY_FACTOR = 1.25
        key = jax.random.key(seed)
        ks = jax.random.split(key, 5)
        B, L, D, F, E = (8, 128, 256, 1024, 8)
        h = jax.random.normal(ks[0], (B, L, D), dtype=jnp.float32)
        gate_w = jax.random.normal(ks[1], (D, E), dtype=jnp.float32) * 0.02
        gate_b = jnp.zeros((E,), dtype=jnp.float32)
        w1 = jax.random.normal(ks[2], (E, D, F), dtype=jnp.float32) * (1.0 / math.sqrt(D))
        b1 = jnp.zeros((E, F), dtype=jnp.float32)
        w2 = jax.random.normal(ks[3], (E, F, D), dtype=jnp.float32) * (1.0 / math.sqrt(F))
        b2 = jnp.zeros((E, D), dtype=jnp.float32)
        return {'h': h, 'gate_w': gate_w, 'gate_b': gate_b, 'w1': w1, 'b1': b1, 'w2': w2, 'b2': b2}
    _L0_ffn_all = _L0_ffn_setup()
    _L0_ffn_in = {k: v for k, v in _L0_ffn_all.items() if k in ('gate_w', 'gate_b', 'w1', 'b1', 'w2', 'b2')}
    del _L0_ffn_all
    return {'x': x, 'src': src, 'dst': dst, 'edge_weight': edge_weight, 'L0_ffn_gate_w': _L0_ffn_in['gate_w'], 'L0_ffn_gate_b': _L0_ffn_in['gate_b'], 'L0_ffn_w1': _L0_ffn_in['w1'], 'L0_ffn_b1': _L0_ffn_in['b1'], 'L0_ffn_w2': _L0_ffn_in['w2'], 'L0_ffn_b2': _L0_ffn_in['b2']}

def reference(x, src, dst, edge_weight, L0_ffn_gate_w, L0_ffn_gate_b, L0_ffn_w1, L0_ffn_b1, L0_ffn_w2, L0_ffn_b2):
    import jax
    import jax.numpy as jnp

    def _L0_gnn_ref(m, row, col, vals):
        import jax, jax.numpy as jnp
        import numpy as np
        N = 50000
        NNZ = 12500
        D = 256
        H = m.astype(jnp.float16)
        v = vals.astype(jnp.float16)
        msgs = H[col] * v[:, None]
        out = jax.ops.segment_sum(msgs, row, num_segments=N)
        return out.astype(m.dtype)

    def _L0_ffn_ref(h, gate_w, gate_b, w1, b1, w2, b2):
        import math
        import jax, jax.numpy as jnp
        import numpy as np
        CAPACITY_FACTOR = 1.25
        B, L, D = h.shape
        E = gate_w.shape[1]
        T = B * L
        C = max(1, math.ceil(CAPACITY_FACTOR * T / E))
        x = h.reshape(T, D)
        logits = x @ gate_w + gate_b
        probs = jax.nn.softmax(logits, axis=-1)
        idx = jnp.argmax(probs, axis=-1)
        prb = jnp.take_along_axis(probs, idx[:, None], axis=1)[:, 0]
        one_hot = jax.nn.one_hot(idx, E, dtype=jnp.float32)
        pos = (jnp.cumsum(one_hot, axis=0) * one_hot).sum(-1).astype(jnp.int32) - 1
        kept = pos < C
        pos_safe = jnp.where(kept, pos, C)
        buf = jnp.zeros((E, C, D), dtype=h.dtype).at[idx, pos_safe].set(x, mode='drop')
        hmid = jax.nn.relu(jnp.einsum('ecd,edf->ecf', buf, w1) + b1[:, None, :])
        ybuf = jnp.einsum('ecf,efd->ecd', hmid, w2) + b2[:, None, :]
        pos_g = jnp.minimum(pos, C - 1)
        y_tok = ybuf[idx, pos_g] * (prb * kept)[:, None]
        y = y_tok.reshape(B, L, D)
        y = jnp.nan_to_num(y, nan=0.0, posinf=10000.0, neginf=-10000.0)
        return y
    x = x + _L0_gnn_ref(_layernorm(x, axis=-1), src, dst, edge_weight)
    x = x + _L0_ffn_ref(_layernorm(x, axis=-1)[None], L0_ffn_gate_w, L0_ffn_gate_b, L0_ffn_w1, L0_ffn_b1, L0_ffn_w2, L0_ffn_b2)[0]
    return x

_drawn_inputs = setup_inputs


def setup_inputs(seed=0):
    import zlib

    import numpy as np

    out = dict(_drawn_inputs(seed))
    spreads = {'L0_ffn_gate_b': (0.0, 0.1), 'L0_ffn_b1': (0.0, 0.742), 'L0_ffn_b2': (0.0, 0.524)}
    factors = {}
    for name, (base, spread) in spreads.items():
        noise = np.random.default_rng([zlib.crc32(name.encode()), seed]).standard_normal(out[name].shape)
        drawn = base * np.exp(spread * noise) if base else spread * noise
        out[name] = jnp.asarray(drawn.astype(out[name].dtype))
    for name, factor in factors.items():
        out[name] = (out[name] * factor).astype(out[name].dtype)
    return out
```

```python
import math
from contextlib import ExitStack

import concourse.bass as bass
from concourse import mybir

ALU = mybir.AluOpType
ACT = mybir.ActivationFunctionType
AX = mybir.AxisListType
F32 = mybir.dt.float32
F32R = mybir.dt.float32r
F16 = mybir.dt.float16
I32 = mybir.dt.int32
U8 = mybir.dt.uint8

P = 128
G = 8
STEP = G * P
EPS = 1e-5
CAPACITY_FACTOR = 1.25
FLAG = float(1 << 20)

MEAN, RSTD, TOKEN, LOGIT = 256, 257, 258, 259
RING = 4


class Count:

    def __init__(self, base):
        self.base, self.n = base, 0

    def inc(self):
        self.n += 1
        return 1

    def now(self):
        return self.base + self.n


def steps(eng, total, unroll, body):
    for r in range(unroll):
        body(0, r)
    with eng.Fori(1, total // unroll) as i:
        for r in range(unroll):
            body(i, r)
    for r in range(total % unroll):
        body(total // unroll, r)


def edge_and_constants(nc, ctx, t):
    x, src, dst, weight = t["x"], t["src"], t["dst"], t["weight"]
    agg, slots = t["agg"], t["slots"]
    N, D = x.shape
    M = src.shape[0]
    S = -(-M // STEP)
    LAST = S - 1
    REPEATED = S * STEP - M
    assert REPEATED < STEP and LAST % 2 == 0
    W = slots.shape[1]

    def base_of(i, r):
        return M - STEP if (isinstance(i, int) and 2 * i + r == LAST) else i * (2 * STEP) + r * STEP

    def sb(name, shape, dt):
        return ctx.enter_context(nc.sbuf_tensor(name, shape, dt))

    def sem(name):
        return ctx.enter_context(nc.semaphore(name))

    zeros = sb("zeros16", [P, 16 * D], F16)
    blank = sb("blank_slots", [P, G, W], F32)
    src_row = sb("src_row", [P, 2, STEP], I32)
    src_col = sb("src_col", [P, 2, G], I32)
    dst_col = sb("dst_col", [P, 2, G], I32)
    w_col = sb("w_col", [P, 2, G], F32)
    w16 = sb("w16", [P, 2, G], F16)
    w32 = sb("w32", [P, 2, G], F32)
    srcf = sb("srcf", [P, 2, G], F32)
    rows = sb("rows", [P, 2, G, D], F32)
    same = sb("same", [P, 2, G, STEP], F16)
    earlier = sb("earlier", [P, 2, G, P], F16)
    stats = sb("e_stats", [P, G, 6], F32)
    mv = sb("e_mv", [P, 2, G, 2], F32)
    std = sb("e_std", [P, 2, G], F32)
    rstd = sb("e_rstd", [P, G], F32)
    msg = sb("msg", [P, 2, G, D], F16)
    norm16 = sb("norm16", [P, G, D], F16)
    sums = sb("sums", [P, 2, G, D], F16)
    spare_i = sb("spare_i", [P, G], I32)
    spare = sb("spare", [P, G], F32)
    shift = sb("shift", [P, G], F32)
    target = sb("target", [P, 2, G], I32)
    ones, before, ident, eps = t["ones"], t["before"], t["ident"], t["eps"]

    ps_sum = ctx.enter_context(nc.psum_tensor("ps_sum", [P, G, D], F32))
    ps_cnt = ctx.enter_context(nc.psum_tensor("ps_cnt", [P, 512], F32))

    set_up = sem("set_up")
    pool_set = sem("pool_set")
    agg_zeroed = sem("agg_zeroed")
    slots_blank = sem("slots_blank")
    idx_loaded = [sem(f"idx_loaded{r}") for r in range(2)]
    gathered = [sem(f"gathered{r}") for r in range(2)]
    added = [sem(f"added{r}") for r in range(2)]
    masks_ready = sem("masks_ready")
    stats_ready = sem("e_stats_ready")
    std_ready = sem("e_std_ready")
    msg_ready = sem("msg_ready")
    counted = sem("counted")
    summed = sem("summed")
    sums_out = sem("sums_out")
    edge_done = sem("edge_done")
    step = sem("e_step")

    BANKS = G * D // 512
    PER_BANK = G // BANKS
    row_view = lambda ap: ap.rearrange("(p c) -> p c", c=G)
    agg_v = agg.rearrange("(p b r) d -> b p (r d)", p=P, r=16)
    slots_v = slots.rearrange("(p b r) w -> b p r w", p=P, r=G)

    with nc.Block() as block:

        @block.sync
        def _(sp):
            def load(i, r):
                s = 2 * i + r
                if not (isinstance(i, int) and i == 0):
                    sp.wait_ge(edge_done, s - 1)
                b = base_of(i, r)
                sp.dma_start(dst_col[:, r, :], row_view(dst[bass.ds(b, STEP)])).then_inc(idx_loaded[r], 16)
                sp.dma_start(src_col[:, r, :], row_view(src[bass.ds(b, STEP)])).then_inc(idx_loaded[r], 16)
                sp.dma_start(w_col[:, r, :], row_view(weight[bass.ds(b, STEP)])).then_inc(idx_loaded[r], 16)
                sp.dma_start(src_row[:, r, :], src[bass.ds(b, STEP)].partition_broadcast(P))\
                    .then_inc(idx_loaded[r], 16)
            steps(sp, S, 2, load)

        @block.gpsimd
        def _(pool):
            pool.memset(before[:], 1.0).then_inc(pool_set, 1)
            pool.memset(ident[:], 0.0).then_inc(pool_set, 1)
            pool.iota(spare_i[:], [[P, G]], base=N, channel_multiplier=1).then_inc(pool_set, 1)
            pool.wait_ge(pool_set, 3)
            pool.affine_select(out=before[:], in_=before[:], compare_op=ALU.is_gt, fill=0.0, base=0,
                               pattern=[[1, P]], channel_multiplier=-1).then_inc(pool_set, 1)
            pool.affine_select(out=ident[:], in_=ident[:], compare_op=ALU.not_equal, fill=1.0, base=0,
                               pattern=[[-1, P]], channel_multiplier=1).then_inc(pool_set, 1)

            def gather(i, r):
                pool.wait_ge(idx_loaded[r], 64 * (i + 1))
                pool.nop(nofuse=True)
                if not (isinstance(i, int) and i == 0):
                    pool.wait_ge(edge_done, 2 * i + r - 1)
                    pool.nop(nofuse=True)
                for c in range(G):
                    pool.indirect_dma_start(
                        out=rows[:, r, c, :], out_offset=None, in_=x[:, :],
                        in_offset=bass.IndirectOffsetOnAxis(ap=dst_col[:, r, c:c + 1], axis=0),
                    ).then_inc(gathered[r], 16)

            def scatter(i, r):
                s = 2 * i + r
                pool.wait_ge(edge_done, s + 1)
                pool.wait_ge(sums_out, BANKS * (s + 1))
                pool.nop(nofuse=True)
                if isinstance(i, int) and s == 0:
                    pool.wait_ge(agg_zeroed, 16 * agg_v.shape[0])
                else:
                    pool.wait_ge(added[1 - r], 16 * G * (i + r))
                    pool.nop(nofuse=True)
                for c in range(G):
                    pool.indirect_dma_start(
                        out=agg[:, :], out_offset=bass.IndirectOffsetOnAxis(ap=target[:, r, c:c + 1], axis=0),
                        in_=sums[:, r, c, :], in_offset=None, compute_op=ALU.add,
                    ).then_inc(added[r], 16)

            gather(0, 0)
            gather(0, 1)
            scatter(0, 0)
            gather(1, 0)
            scatter(0, 1)
            with pool.Fori(1, S // 2) as i:
                gather(i, 1)
                scatter(i, 0)
                gather(i + 1, 0)
                scatter(i, 1)
            scatter(S // 2, 0)
            pool.wait_ge(added[0], 16 * G * (S // 2 + 1))
            pool.wait_ge(added[1], 16 * G * (S // 2))

        @block.scalar
        def _(act):
            act.wait_ge(set_up, 2)
            with act.Fori(0, agg_v.shape[0]) as b:
                act.dma_start(agg_v[b], zeros[:]).then_inc(agg_zeroed, 16)
            act.wait_ge(set_up, 3)
            FEW = slots_v.shape[0] // S

            def body(i, r):
                s = 2 * i + r
                act.wait_ge(stats_ready, s + 1)
                for k in range(FEW):
                    act.dma_start(slots_v[i * (2 * FEW) + (r * FEW + k)], blank[:]).then_inc(slots_blank, 16)
                act.activation(std[:, r, :], mv[:, r, :, 1], ACT.Sqrt, bias=eps[:, 0:1]).then_inc(std_ready, 1)
                if not (isinstance(i, int) and i == 0):
                    act.wait_ge(added[r], 16 * G * i)
                for b in range(BANKS):
                    act.wait_ge(summed, BANKS * s + b + 1)
                    part = slice(b * PER_BANK, (b + 1) * PER_BANK)
                    act.activation(sums[:, r, part, :], ps_sum[:, part, :], ACT.Copy).then_inc(sums_out, 1)
            steps(act, S, 2, body)
            for b in range(FEW * S, slots_v.shape[0]):
                act.dma_start(slots_v[b], blank[:]).then_inc(slots_blank, 16)
            act.wait_ge(slots_blank, 16 * slots_v.shape[0])

        @block.vector
        def _(v):
            v.memset(zeros[:], 0.0).then_inc(set_up, 1)
            v.memset(eps[:], EPS).then_inc(set_up, 1)
            v.memset(blank[:], 0.0).then_inc(step, 1)
            v.memset(ones[:], 1.0)
            v.wait_ge(step, 1)
            v.memset(blank[:, :, TOKEN:TOKEN + 1].bitcast(I32), 1 << 20).then_inc(set_up, 1)
            v.wait_ge(pool_set, 5)
            v.tensor_copy(spare[:], spare_i[:]).then_inc(step, 1)
            v.wait_ge(step, 2)
            SET, PER = 2, 8

            def body(i, r):
                s = 2 * i + r
                n = Count(s * PER + SET)
                v.wait_ge(idx_loaded[r], 64 * (i + 1))
                v.tensor_copy(srcf[:, r, :], src_col[:, r, :])
                v.tensor_copy(w16[:, r, :], w_col[:, r, :]).then_inc(step, n.inc())
                v.wait_ge(step, n.now())
                v.tensor_copy(w32[:, r, :], w16[:, r, :]).then_inc(step, n.inc())
                if isinstance(i, int) and s == LAST and REPEATED:
                    assert REPEATED % G == 0
                    v.wait_ge(step, n.now())
                    v.memset(w32[0:REPEATED // G, r, :], 0.0).then_inc(step, 1)
                    n.base += 1
                if not (isinstance(i, int) and i == 0):
                    v.wait_ge(summed, BANKS * (s - 1))
                for c in range(G):
                    last = v.tensor_scalar(same[:, r, c, :], src_row[:, r, :], srcf[:, r, c:c + 1], None,
                                           ALU.is_equal)
                last.then_inc(step, n.inc())
                v.wait_ge(step, n.now())
                for c in range(G):
                    last = v.tensor_tensor(earlier[:, r, c, :],
                                           same[:, r, c, :].rearrange("j (p a) -> j a p", a=G)[:, c, :],
                                           before[:], ALU.mult)
                last.then_inc(masks_ready, 1)
                v.wait_ge(gathered[r], 16 * G * (i + 1))
                for c in range(G):
                    last = v.bn_stats(stats[:, c, :], rows[:, r, c, :])
                last.then_inc(step, n.inc())
                v.wait_ge(step, n.now())
                v.nop(nofuse=True)
                for c in range(G):
                    last = v.bn_aggr(mv[:, r, c, :], stats[:, c, :])
                last.then_inc(stats_ready, 1)
                v.tensor_tensor(shift[:], spare[:], srcf[:, r, :], ALU.subtract).then_inc(step, n.inc())
                v.wait_ge(std_ready, s + 1)
                v.reciprocal(rstd[:], std[:, r, :]).then_inc(step, n.inc())
                v.wait_ge(step, n.now())
                for c in range(G):
                    last = v.tensor_scalar(norm16[:, c, :], rows[:, r, c, :], mv[:, r, c, 0:1], rstd[:, c:c + 1],
                                           ALU.subtract, ALU.mult)
                last.then_inc(step, n.inc())
                v.wait_ge(step, n.now())
                for c in range(G):
                    last = v.tensor_scalar(msg[:, r, c, :], norm16[:, c, :], w32[:, r, c:c + 1], None, ALU.mult)
                last.then_inc(msg_ready, 1)
                v.wait_ge(counted, s + 1)
                v.scalar_tensor_tensor(out=shift[:], in0=ps_cnt[:, 0:G], scalar=0.5, in1=shift[:],
                                       op0=ALU.is_gt, op1=ALU.mult).then_inc(step, n.inc())
                v.wait_ge(step, n.now())
                if not (isinstance(i, int) and i == 0):
                    v.wait_ge(added[r], 16 * G * i)
                v.tensor_tensor(target[:, r, :], shift[:], srcf[:, r, :], ALU.add).then_inc(edge_done, 1)
                assert n.n == PER, n.n
            steps(v, S, 2, body)

        @block.tensor
        def _(pe):
            def body(i, r):
                s = 2 * i + r
                seen = lambda b, c: same[:, r, b, :].rearrange("j (p a) -> j a p", a=G)[:, c, :]
                pe.wait_ge(masks_ready, s + 1)
                if not (isinstance(i, int) and s == 0):
                    pe.wait_ge(edge_done, s)
                for c in range(G):
                    for b in range(c):
                        pe.matmul(ps_cnt[:, c:c + 1], seen(b, c), ones[:, 0:1], start=(b == 0), stop=False)
                    last = pe.matmul(ps_cnt[:, c:c + 1], earlier[:, r, c, :], ones[:, 0:1],
                                     start=(c == 0), stop=True)
                last.then_inc(counted, 1)
                pe.wait_ge(msg_ready, s + 1)
                for k in range(BANKS):
                    if not (isinstance(i, int) and s == 0):
                        pe.wait_ge(sums_out, BANKS * (s - 1) + k + 1)
                    for c in range(k * PER_BANK, (k + 1) * PER_BANK):
                        for b in range(G):
                            last = pe.matmul(ps_sum[:, c, :], seen(b, c), msg[:, r, b, :],
                                             start=(b == 0), stop=(b == G - 1))
                    last.then_inc(summed, 1)
            steps(pe, S, 2, body)


def route_tokens(nc, ctx, t):
    x, agg, slots, out = t["x"], t["agg"], t["slots"], t["out"]
    gate_w, gate_b = t["gate_w"], t["gate_b"]
    N, D = x.shape
    E = gate_w.shape[1]
    KD = D // P
    W = slots.shape[1]
    C, QUEUE = t["C"], t["QUEUE"]
    S = -(-N // STEP)
    LAST = S - 1
    REPEATED = S * STEP - N
    assert LAST % RING == 0

    def base_of(i, r):
        s = RING * i + r
        return N - STEP if (isinstance(i, int) and s == LAST) else i * (RING * STEP) + r * STEP

    def sb(name, shape, dt):
        return ctx.enter_context(nc.sbuf_tensor(name, shape, dt))

    def sem(name):
        return ctx.enter_context(nc.semaphore(name))

    xt = sb("xt", [P, 2, G, D], F32)
    at = sb("at", [P, 2, G, D], F16)
    pay = sb("pay", [P, RING, G, W], F32)
    h = sb("h", [P, 2, G, D], F32)
    hT = sb("hT", [P, G * KD, P], F32)
    gw = sb("gw", [P, KD, E], F32)
    gb = sb("gb", [P, E], F32)
    stats = sb("t_stats", [P, G, 6], F32)
    mv = sb("t_mv", [P, 2, G, 2], F32)
    std = sb("t_std", [P, 2, G], F32)
    shift = sb("t_shift", [P, 2, G], F32)
    token_i = sb("token_i", [P, G], I32)
    token = sb("token", [P, G], F32)
    expert_i = sb("expert_i", [P, E], I32)
    expert = sb("expert", [P, E], F32)
    prefer = sb("prefer", [P, E], F32)
    limit = sb("limit", [P, E], F32)
    fresh = sb("fresh", [P, G], F16)
    lg = sb("lg", [P, G, E], F32)
    cand = sb("cand", [P, G, E], F32)
    top = sb("top", [P, G], F32)
    best = sb("best", [P, G], F32)
    hot = sb("hot", [P, 2, G, E], F16)
    place = sb("place", [P, 2, G + 1, E], F32)
    kept_hot = sb("kept_hot", [P, G, E], F32)
    own = sb("own", [P, G, E], F32)
    kept = sb("kept", [P, G], F32)
    where = sb("where", [P, G], F32)
    slot_i = sb("slot_i", [P, RING, G], I32)
    ones, before, ident, eps = t["ones"], t["before"], t["ident"], t["eps"]

    ps_T = ctx.enter_context(nc.psum_tensor("ps_T", [P, G * KD, P], F32))
    ps_L = ctx.enter_context(nc.psum_tensor("ps_L", [P, 512], F32))
    ps_R = ctx.enter_context(nc.psum_tensor("ps_R", [P, 512], F32))
    logits = ps_L[:, 0:G * E].rearrange("p (g e) -> p g e", g=G)
    ranks = ps_R[:, 0:(G + 1) * E].rearrange("p (g e) -> p g e", g=G + 1)

    consts = sem("t_consts")
    pool_set = sem("t_pool_set")
    loaded = [sem(f"t_loaded{r}") for r in range(2)]
    x1_ready = sem("x1_ready")
    stats_ready = sem("t_stats_ready")
    std_ready = sem("t_std_ready")
    norm_ready = sem("norm_ready")
    h_ready = sem("h_ready")
    turned = sem("turned")
    hT_ready = sem("hT_ready")
    gated = sem("gated")
    hot_ready = sem("hot_ready")
    ranked = sem("ranked")
    slot_ready = sem("slot_ready")
    out_written = [sem(f"out_written{r}") for r in range(RING)]
    sent = [sem(f"sent{r}") for r in range(RING)]
    step = sem("t_step")
    step_b = sem("t_step_b")

    BANKS = G * KD * P // 512
    PER_BANK = G * KD // BANKS

    with nc.Block() as block:

        @block.sync
        def _(sp):
            sp.dma_start(gw[:], gate_w.rearrange("(k p) e -> p k e", p=P)).then_inc(consts, 16)
            sp.dma_start(gb[:], gate_b.partition_broadcast(P)).then_inc(consts, 16)

            def load(i, r):
                s = RING * i + r
                if not (isinstance(i, int) and s < 2):
                    sp.wait_ge(x1_ready, s - 1)
                b = base_of(i, r)
                sp.dma_start(xt[:, r % 2], x[bass.ds(b, STEP), :].rearrange("(g p) d -> p g d", p=P))\
                    .then_inc(loaded[r % 2], 16)
                sp.dma_start(at[:, r % 2], agg[bass.ds(b, STEP), :].rearrange("(g p) d -> p g d", p=P))\
                    .then_inc(loaded[r % 2], 16)

            def store(i, r, b):
                sp.wait_ge(x1_ready, RING * i + r + 1)
                sp.dma_start(out[bass.ds(b, STEP), :].rearrange("(g p) d -> p g d", p=P), pay[:, r, :, 0:D])\
                    .then_inc(out_written[r], 16)

            load(0, 0)
            for r in range(1, RING):
                load(0, r)
                store(0, r - 1, base_of(0, r - 1))
            with sp.Fori(1, S // RING) as i:
                for r in range(RING):
                    load(i, r)
                    if r:
                        store(i, r - 1, base_of(i, r - 1))
                    else:
                        store(i - 1, RING - 1, base_of(i - 1, RING - 1))
            n = S // RING
            load(n, 0)
            store(n - 1, RING - 1, base_of(n - 1, RING - 1))
            sp.wait_ge(out_written[RING - 1], 16 * n)
            store(n, 0, base_of(n, 0))
            for r in range(RING):
                sp.wait_ge(out_written[r], 16 * (n + (r == 0)))

        @block.gpsimd
        def _(pool):
            pool.iota(token_i[:], [[P, G]], base=0, channel_multiplier=1).then_inc(pool_set, 1)
            pool.iota(expert_i[:], [[1, E]], base=0, channel_multiplier=0).then_inc(pool_set, 1)
            pool.memset(fresh[:], 1.0).then_inc(pool_set, 1)
            pool.wait_ge(pool_set, 3)
            pool.affine_select(out=fresh[:], in_=fresh[:], compare_op=ALU.is_ge, fill=0.0, base=-REPEATED,
                               pattern=[[P, G]], channel_multiplier=1).then_inc(pool_set, 1)

            def body(i, r):
                pool.wait_ge(slot_ready, RING * i + r + 1)
                pool.nop(nofuse=True)
                for g in range(G):
                    pool.indirect_dma_start(
                        out=slots[:, :], out_offset=bass.IndirectOffsetOnAxis(ap=slot_i[:, r, g:g + 1], axis=0),
                        in_=pay[:, r, g, :], in_offset=None, bounds_check=E * QUEUE - 1, oob_is_err=False,
                    ).then_inc(sent[r], 16)
            steps(pool, S, RING, body)
            for r in range(RING):
                pool.wait_ge(sent[r], 16 * G * (S // RING + (r < S % RING)))

        @block.scalar
        def _(act):
            def body(i, r):
                s = RING * i + r
                q = r % 2
                act.wait_ge(stats_ready, s + 1)
                act.activation(std[:, q, :], mv[:, q, :, 1], ACT.Sqrt, bias=eps[:, 0:1]).then_inc(std_ready, 1)
                act.wait_ge(norm_ready, s + 1)
                if not (isinstance(i, int) and s < 2):
                    act.wait_ge(turned, BANKS * (s - 1))
                if not (isinstance(i, int) and s < 1):
                    act.wait_ge(gated, s)
                act.nop(nofuse=True)

                def copy(k):
                    act.wait_ge(turned, BANKS * s + k + 1)
                    part = slice(k * PER_BANK, (k + 1) * PER_BANK)
                    act.activation(hT[:, part, :], ps_T[:, part, :], ACT.Copy).then_inc(hT_ready, 1)

                for k in range(BANKS):
                    for g in range(k * G // BANKS, (k + 1) * G // BANKS):
                        last = act.activation(h[:, q, g, :], pay[:, r, g, 0:D], ACT.Identity,
                                              bias=shift[:, q, g:g + 1], scale=pay[:, r, g, RSTD:RSTD + 1])
                    last.then_inc(h_ready, 1)
                    if k:
                        copy(k - 1)
                copy(BANKS - 1)
            steps(act, S, RING, body)

        @block.tensor
        def _(pe):
            def rank(i, r):
                s = RING * i + r
                q = r % 2
                pe.wait_ge(hot_ready, s + 1)
                if not (isinstance(i, int) and s < 1):
                    pe.wait_ge(slot_ready, s)
                pe.matmul(ranks[:, 0:G, :], before[:], hot[:, q], start=True, stop=False, skip_group_check=True)
                for g in range(G):
                    last = pe.matmul(ranks[:, g + 1:G + 1, :], ones[:],
                                     hot[:, q, g, :].unsqueeze(1).broadcast_to([P, G - g, E]),
                                     start=False, stop=(g == G - 1), skip_group_check=True)
                last.then_inc(ranked, 1)

            def gate(s, k, i):
                pe.wait_ge(hT_ready, BANKS * s + k + 1)
                if not (isinstance(i, int) and isinstance(s, int) and s < 1):
                    pe.wait_ge(hot_ready, s)
                else:
                    pe.wait_ge(consts, 32)
                for g in range(k * G // BANKS, (k + 1) * G // BANKS):
                    for kd in range(KD):
                        last = pe.matmul(logits[:, g, :], hT[:, g * KD + kd, :], gw[:, kd, :],
                                         start=(kd == 0), stop=(kd == KD - 1))
                if k == BANKS - 1:
                    last.then_inc(gated, 1)

            def body(i, r):
                s = RING * i + r
                q = r % 2
                if not (isinstance(i, int) and s < 1):
                    rank(*((i, r - 1) if r else (i - 1, RING - 1)))
                for k in range(BANKS):
                    pe.wait_ge(h_ready, BANKS * s + k + 1)
                    if not (isinstance(i, int) and s < 1):
                        pe.wait_ge(hT_ready, BANKS * (s - 1) + k + 1)
                    for n in range(k * PER_BANK, (k + 1) * PER_BANK):
                        g, kd = divmod(n, KD)
                        last = pe.transpose(ps_T[:, n, :], h[:, q, g, kd * P:(kd + 1) * P], ident[:])
                    last.then_inc(turned, 1)
                    if k:
                        gate(s, k - 1, i)
                gate(s, BANKS - 1, i)
            steps(pe, S, RING, body)
            rank(LAST // RING, 0)

        @block.vector
        def _(v):
            v.wait_ge(pool_set, 4)
            v.tensor_copy(token[:], token_i[:])
            v.tensor_copy(expert[:], expert_i[:]).then_inc(step, 1)
            v.wait_ge(step, 1)
            v.tensor_scalar(prefer[:], expert[:], -1.0, float(E), ALU.mult, ALU.add)
            v.tensor_scalar(limit[:], expert[:], float(QUEUE), float(C), ALU.mult, ALU.add)
            v.tensor_scalar(place[:, 1, G, :], expert[:], float(QUEUE), None, ALU.mult).then_inc(step, 1)
            v.wait_ge(step, 2)
            v.wait_ge(consts, 32)
            SET, PER_A, PER_B = 2, 4, 12

            def statistics(i, r, n):
                s = RING * i + r
                q = r % 2
                last_step = isinstance(i, int) and s == LAST
                v.wait_ge(loaded[q], 32 * ((RING // 2) * i + r // 2 + 1))
                if not (isinstance(i, int) and i == 0):
                    v.wait_ge(sent[r], 16 * G * i)
                    v.wait_ge(out_written[r], 16 * i)
                v.tensor_tensor(pay[:, r, :, 0:D], xt[:, q], at[:, q], ALU.add).then_inc(x1_ready, 1)
                v.wait_ge(x1_ready, s + 1)
                for g in range(G):
                    last = v.bn_stats(stats[:, g, :], pay[:, r, g, 0:D])
                last.then_inc(step, n.inc())
                if last_step:
                    v.tensor_scalar(token[:], token[:], -float(REPEATED), None, ALU.add).then_inc(step, n.inc())
                else:
                    v.engine_nop().then_inc(step, n.inc())
                v.wait_ge(step, n.now())
                v.nop(nofuse=True)
                for g in range(G):
                    last = v.bn_aggr(mv[:, q, g, :], stats[:, g, :])
                last.then_inc(stats_ready, 1)

            def scales(i, r, n):
                s = RING * i + r
                q = r % 2
                v.tensor_copy(pay[:, r, :, TOKEN].bitcast(I32), token[:]).then_inc(step, n.inc())
                v.wait_ge(step, n.now())
                v.tensor_scalar(token[:], token[:], float(STEP), None, ALU.add)
                v.tensor_copy(pay[:, r, :, MEAN], mv[:, q, :, 0])
                v.wait_ge(std_ready, s + 1)
                v.reciprocal(pay[:, r, :, RSTD], std[:, q, :]).then_inc(step, n.inc())
                v.wait_ge(step, n.now())
                v.scalar_tensor_tensor(out=shift[:, q, :], in0=mv[:, q, :, 0], scalar=-1.0,
                                       in1=pay[:, r, :, RSTD], op0=ALU.mult, op1=ALU.mult)\
                    .then_inc(norm_ready, 1)
                assert n.n == PER_A, n.n

            def choice(i, r, n):
                s = RING * i + r
                q = r % 2
                last_step = isinstance(i, int) and s == LAST
                v.wait_ge(gated, s + 1)
                v.tensor_tensor(lg[:], logits, gb[:].unsqueeze(1).broadcast_to([P, G, E]), ALU.add)\
                    .then_inc(step_b, n.inc())
                v.wait_ge(step_b, n.now())
                v.tensor_reduce(top[:], lg[:], AX.X, ALU.max).then_inc(step_b, n.inc())
                v.wait_ge(step_b, n.now())
                less = pay[:, r, :, LOGIT:LOGIT + E]
                v.tensor_tensor(less, lg[:], top[:].unsqueeze(2).broadcast_to([P, G, E]), ALU.subtract)\
                    .then_inc(step_b, n.inc())
                v.wait_ge(step_b, n.now())
                v.scalar_tensor_tensor(out=cand[:], in0=less, scalar=0.0,
                                       in1=prefer[:].unsqueeze(1).broadcast_to([P, G, E]),
                                       op0=ALU.is_equal, op1=ALU.mult).then_inc(step_b, n.inc())
                v.wait_ge(step_b, n.now())
                v.tensor_reduce(best[:], cand[:], AX.X, ALU.max).then_inc(step_b, n.inc())
                v.wait_ge(step_b, n.now())
                if last_step:
                    v.tensor_tensor(own[:], cand[:], best[:].unsqueeze(2).broadcast_to([P, G, E]), ALU.is_equal)\
                        .then_inc(step_b, n.inc())
                    v.wait_ge(step_b, n.now())
                    v.tensor_tensor(hot[:, q], own[:], fresh[:].unsqueeze(2).broadcast_to([P, G, E]), ALU.mult)\
                        .then_inc(hot_ready, 1)
                else:
                    v.tensor_tensor(hot[:, q], cand[:], best[:].unsqueeze(2).broadcast_to([P, G, E]), ALU.is_equal)\
                        .then_inc(hot_ready, 1)
                    v.engine_nop().then_inc(step_b, n.inc())

            def slot(i, r, n):
                s = RING * i + r
                q = r % 2
                v.wait_ge(ranked, s + 1)
                v.wait_ge(hot_ready, s + 1)
                v.tensor_tensor(place[:, q], ranks, place[:, 1 - q, G, :].unsqueeze(1).broadcast_to([P, G + 1, E]),
                                ALU.add).then_inc(step_b, n.inc())
                v.wait_ge(step_b, n.now())
                v.tensor_tensor(kept_hot[:], place[:, q, 0:G, :], limit[:].unsqueeze(1).broadcast_to([P, G, E]),
                                ALU.is_lt)
                v.tensor_tensor(own[:], place[:, q, 0:G, :], hot[:, q], ALU.mult).then_inc(step_b, n.inc())
                v.wait_ge(step_b, n.now())
                v.tensor_tensor(kept_hot[:], kept_hot[:], hot[:, q], ALU.mult).then_inc(step_b, n.inc())
                v.tensor_reduce(where[:], own[:], AX.X, ALU.add).then_inc(step_b, n.inc())
                v.wait_ge(step_b, n.now())
                v.tensor_reduce(kept[:], kept_hot[:], AX.X, ALU.add).then_inc(step_b, n.inc())
                v.wait_ge(step_b, n.now())
                v.scalar_tensor_tensor(out=where[:], in0=kept[:], scalar=-FLAG, in1=where[:],
                                       op0=ALU.mult, op1=ALU.add).then_inc(step_b, n.inc())
                v.wait_ge(step_b, n.now())
                v.tensor_scalar(slot_i[:, r, :], where[:], FLAG, None, ALU.add).then_inc(slot_ready, 1)
                assert n.n == PER_B, n.n

            def body(i, r):
                s = RING * i + r
                a, b = Count(s * PER_A + SET), Count((s - 1) * PER_B)
                before_it = (i, r - 1) if r else (i - 1, RING - 1)
                statistics(i, r, a)
                scales(i, r, a)
                if not (isinstance(i, int) and s == 0):
                    choice(*before_it, b)
                    slot(*before_it, b)
            steps(v, S, RING, body)
            b = Count(LAST * PER_B)
            choice(LAST // RING, 0, b)
            slot(LAST // RING, 0, b)


def run_experts(nc, ctx, t):
    slots, out = t["slots"], t["out"]
    w1, b1, w2, b2 = t["w1"], t["b1"], t["w2"], t["b2"]
    E, D, F = w1.shape
    N = out.shape[0]
    W = slots.shape[1]
    QUEUE = t["QUEUE"]
    KD, KF = D // P, F // P
    SUB = 4
    UNIT = SUB * P
    UNITS = -(-QUEUE // UNIT)
    LASTSUB = SUB - (UNITS * UNIT - QUEUE) // P
    ROUNDS = UNITS // RING
    assert UNITS % RING == 0 and (UNITS * UNIT - QUEUE) % P == 0
    WF = KD * F
    PIECE = 2 * WF // UNITS
    assert KF * D == WF and 2 * WF % UNITS == 0
    HUGE = 1e4

    def sb(name, shape, dt):
        return ctx.enter_context(nc.sbuf_tensor(name, shape, dt))

    def sem(name):
        return ctx.enter_context(nc.semaphore(name))

    raw = sb("raw", [P, 2 * WF], F32)
    whi = sb("whi", [P, 2, 2 * WF], F32R)
    wlo = sb("wlo", [P, 2, 2 * WF], F32R)
    b1r = sb("b1r", [E * KF, P], F32)
    b1c = sb("b1c", [P, E * KF], F32)
    b2b = sb("b2b", [P, E, D], F32)
    pay = sb("u_pay", [P, RING, SUB, W], F32)
    hn = sb("hn", [P, SUB, D], F32)
    xhi = sb("xhi", [P, KD, UNIT], F32R)
    xlo = sb("xlo", [P, KD, UNIT], F32R)
    hm = sb("hm", [P, KF, UNIT], F32)
    hhi = sb("hhi", [P, KF, UNIT], F32R)
    hlo = sb("hlo", [P, KF, UNIT], F32R)
    ex = sb("ex", [P, SUB, E], F32)
    total = sb("total", [P, SUB], F32)
    prob = sb("prob", [P, 2, SUB], F32)
    y = sb("y", [P, SUB, D], F32)
    low = sb("low", [P, SUB, D], F32)
    finite = sb("finite", [P, SUB, D], U8)
    yo = sb("yo", [P, 2, SUB, D], F32)
    ident = t["ident"]

    ps_T = ctx.enter_context(nc.psum_tensor("u_T", [P, KD, UNIT], F32))
    ps_H = ctx.enter_context(nc.psum_tensor("u_H", [P, 2, UNIT], F32))
    ps_Y = ctx.enter_context(nc.psum_tensor("u_Y", [P, SUB, 512], F32))

    consts = sem("u_consts")
    b1_turned = sem("b1_turned")
    b1_ready = sem("b1_ready")
    raw_loaded = sem("raw_loaded")
    first_split = sem("first_split")
    split = sem("split")
    pay_loaded = [sem(f"pay_loaded{r}") for r in range(RING)]
    y_sent = [sem(f"y_sent{r}") for r in range(RING)]
    hn_ready = sem("hn_ready")
    ex_ready = sem("ex_ready")
    turned = sem("u_turned")
    xhi_ready = sem("xhi_ready")
    x_ready = sem("x_ready")
    first_done = sem("first_done")
    relu_done = sem("relu_done")
    hhi_ready = sem("hhi_ready")
    hid_ready = sem("hid_ready")
    second_done = sem("second_done")
    y_read = sem("y_read")
    y_ready = sem("y_ready")
    step = sem("u_step")

    w1_at = lambda w, b, k, f: w[:, b, k * F + f * P:k * F + (f + 1) * P]
    w2_at = lambda w, b, f: w[:, b, WF + f * D:WF + (f + 1) * D]

    def subs(r, tail):
        return LASTSUB if tail else SUB

    def sent_before(e, i, r):
        per_expert = 16 * (SUB * ROUNDS - (SUB - LASTSUB if r == RING - 1 else 0))
        return per_expert * e + 16 * SUB * i

    def experts(eng, body):
        body(0, 0)
        with eng.Fori(0, E // 2 - 1) as q:
            body(2 * q + 1, 1)
            body(2 * q + 2, 0)
        body(E - 1, 1)

    def units(eng, e, body):
        start = 0
        if isinstance(e, int) and e == 0:
            for r in range(RING):
                body(0, r, False)
            start = 1
        with eng.Fori(start, ROUNDS - 1) as i:
            for r in range(RING):
                body(i, r, False)
        for r in range(RING):
            body(ROUNDS - 1, r, r == RING - 1)

    def following(e, i, r, tail):
        if tail:
            return e + 1, 0, 0, False
        if r == RING - 1:
            return e, i + 1, 0, False
        return e, i, r + 1, r + 1 == RING - 1 and isinstance(i, int) and i == ROUNDS - 1

    is_first = lambda e, i, r: isinstance(e, int) and isinstance(i, int) and e == 0 and i == 0
    is_last = lambda e, i, r: isinstance(e, int) and isinstance(i, int) and e == E - 1 and i == ROUNDS - 1 and r == RING - 1

    with nc.Block() as block:

        @block.sync
        def _(sp):
            sp.dma_start(b1r[:], b1.rearrange("e (k p) -> (e k) p", p=P)).then_inc(consts, 16)
            sp.dma_start(b2b[:], b2.partition_broadcast(P)).then_inc(consts, 16)

            def expert(e, buf):
                def unit(i, r, tail):
                    n = subs(r, tail)
                    if not is_first(e, i, r):
                        sp.wait_ge(y_sent[r], sent_before(e, i, r))
                    at = e * QUEUE + i * (RING * UNIT) + r * UNIT
                    sp.dma_start(pay[:, r, 0:n, :],
                                 slots[bass.ds(at, n * P), :].rearrange("(s p) w -> p s w", p=P))\
                        .then_inc(pay_loaded[r], 16)
                units(sp, e, unit)
            experts(sp, expert)

        @block.gpsimd
        def _(pool):
            def expert(e, buf):
                more = not (isinstance(e, int) and e == E - 1)

                def unit(i, r, tail):
                    u = e * UNITS + i * RING + r
                    if more:
                        pool.wait_ge(raw_loaded, 32 * (e + 2))
                        pool.nop(nofuse=True)
                        piece = bass.ds(i * (RING * PIECE) + r * PIECE, PIECE)
                        pool.tensor_copy(whi[:, 1 - buf, piece], raw[:, piece]).then_inc(split, 1)
                        pool.wait_ge(split, 2 * u + 1)
                        pool.nop(nofuse=True)
                        pool.tensor_tensor(wlo[:, 1 - buf, piece], raw[:, piece], whi[:, 1 - buf, piece].bitcast(F32),
                                           ALU.subtract).then_inc(split, 1)
                    pool.wait_ge(y_ready, u + 1)
                    pool.nop(nofuse=True)
                    for s in range(subs(r, tail)):
                        pool.indirect_dma_start(
                            out=out[:, :],
                            out_offset=bass.IndirectOffsetOnAxis(ap=pay[:, r, s, TOKEN:TOKEN + 1].bitcast(I32), axis=0),
                            in_=yo[:, r % 2, s, :], in_offset=None, bounds_check=N - 1, oob_is_err=False,
                        ).then_inc(y_sent[r], 16)
                units(pool, e, unit)
            experts(pool, expert)
            for r in range(RING):
                pool.wait_ge(y_sent[r], sent_before(E, 0, r))

        @block.scalar
        def _(act):
            def load_weights(e):
                act.dma_start(raw[:, 0:WF].rearrange("p (k f) -> p k f", k=KD),
                              w1[bass.ds(e, 1)].rearrange("o (k p) f -> (o p) k f", p=P)).then_inc(raw_loaded, 16)
                act.dma_start(raw[:, WF:2 * WF].rearrange("p (k d) -> p k d", k=KF),
                              w2[bass.ds(e, 1)].rearrange("o (k p) d -> (o p) k d", p=P)).then_inc(raw_loaded, 16)

            def inputs(e, i, r, tail, u):
                n = subs(r, tail)
                act.wait_ge(hn_ready, u + 1)
                act.activation(ex[:, 0:n, :], pay[:, r, 0:n, LOGIT:LOGIT + E], ACT.Exp).then_inc(ex_ready, 1)
                act.wait_ge(turned, u + 1)
                act.activation(xhi[:, :, 0:n * P], ps_T[:, :, 0:n * P], ACT.Copy).then_inc(xhi_ready, 1)

            load_weights(0)

            def expert(e, buf):
                more = not (isinstance(e, int) and e == E - 1)
                if more:
                    if isinstance(e, int) and e == 0:
                        act.wait_ge(first_split, 2)
                    else:
                        act.wait_ge(split, e * (2 * UNITS))
                    load_weights(e + 1)

                def unit(i, r, tail):
                    u = e * UNITS + i * RING + r
                    m = subs(r, tail) * P
                    for f in range(KF):
                        act.wait_ge(first_done, KF * u + f + 1)
                        if not (is_first(e, i, r) and r == 0):
                            act.wait_ge(hid_ready, KF * (u - 1) + f + 1)
                        act.nop(nofuse=True)
                        act.activation(hm[:, f, 0:m], ps_H[:, f % 2, 0:m], ACT.Relu,
                                       bias=b1c[:, bass.ds(e * KF + f, 1)]).then_inc(relu_done, 1)
                        act.wait_ge(relu_done, KF * u + f + 1)
                        act.activation(hhi[:, f, 0:m], hm[:, f, 0:m], ACT.Copy).then_inc(hhi_ready, 1)
                    if not is_last(e, i, r):
                        inputs(*following(e, i, r, tail), u + 1)
                units(act, e, unit)
            act.wait_ge(b1_ready, 1)
            inputs(0, 0, 0, False, 0)
            experts(act, expert)

        @block.vector
        def _(v):
            v.wait_ge(b1_turned, 1)
            v.tensor_copy(b1c[:], ps_T[:, 0, 0:E * KF]).then_inc(b1_ready, 1)
            v.wait_ge(raw_loaded, 32)
            v.tensor_copy(whi[:, 0, :], raw[:]).then_inc(first_split, 1)
            v.wait_ge(first_split, 1)
            v.tensor_tensor(wlo[:, 0, :], raw[:], whi[:, 0, :].bitcast(F32), ALU.subtract).then_inc(first_split, 1)
            v.wait_ge(consts, 32)
            PER = 8

            def normalise(e, i, r, tail, u):
                n = subs(r, tail)
                v.wait_ge(pay_loaded[r], 16 * (ROUNDS * e + i + 1))
                if not is_first(e, i, r) or r > 0:
                    v.wait_ge(turned, u)
                for s in range(n):
                    last = v.tensor_scalar(hn[:, s, :], pay[:, r, s, 0:D], pay[:, r, s, MEAN:MEAN + 1],
                                           pay[:, r, s, RSTD:RSTD + 1], ALU.subtract, ALU.mult)
                last.then_inc(hn_ready, 1)

            def inputs(e, i, r, tail, u, c):
                n = subs(r, tail)
                m = n * P
                v.wait_ge(ex_ready, u + 1)
                v.tensor_reduce(total[:, 0:n], ex[:, 0:n, :], AX.X, ALU.add).then_inc(step, c.inc())
                v.wait_ge(xhi_ready, u + 1)
                v.tensor_tensor(xlo[:, :, 0:m], ps_T[:, :, 0:m], xhi[:, :, 0:m].bitcast(F32), ALU.subtract)\
                    .then_inc(x_ready, 1)
                v.wait_ge(step, c.now())
                v.reciprocal(prob[:, r % 2, 0:n], total[:, 0:n]).then_inc(step, c.inc())

            def expert(e, buf):
                def unit(i, r, tail):
                    n = subs(r, tail)
                    m = n * P
                    u = e * UNITS + i * RING + r
                    c = Count(u * PER + SET)
                    if not is_last(e, i, r):
                        normalise(*following(e, i, r, tail), u + 1)
                    for f in range(KF):
                        v.wait_ge(hhi_ready, KF * u + f + 1)
                        v.tensor_tensor(hlo[:, f, 0:m], hm[:, f, 0:m], hhi[:, f, 0:m].bitcast(F32), ALU.subtract)\
                            .then_inc(hid_ready, 1)
                    if not is_last(e, i, r):
                        inputs(*following(e, i, r, tail), u + 1, c)
                    v.wait_ge(second_done, u + 1)
                    for s in range(n):
                        last = v.tensor_tensor(y[:, s, :], ps_Y[:, s, 0:D], b2b[:, bass.ds(e, 1), :].rearrange("p o d -> p (o d)"),
                                               ALU.add)
                    last.then_inc(y_read, 1)
                    v.wait_ge(y_read, u + 1)
                    for s in range(n):
                        last = v.tensor_scalar(y[:, s, :], y[:, s, :], prob[:, r % 2, s:s + 1], None, ALU.mult)
                    last.then_inc(step, c.inc())
                    v.wait_ge(step, c.now())
                    ya, la, fa, oa = y[:, 0:n, :], low[:, 0:n, :], finite[:, 0:n, :], yo[:, r % 2, 0:n, :]
                    v.tensor_scalar(fa, ya, 0.0, 0.0, ALU.mult, ALU.is_equal)
                    v.tensor_scalar(la, ya, 0.0, -HUGE, ALU.is_lt, ALU.mult).then_inc(step, c.inc())
                    if not is_first(e, i, r) or r > 1:
                        rr = (r - 2) % RING
                        v.wait_ge(y_sent[rr], sent_before(e, i, rr) + (16 * SUB if r >= 2 else 0))
                    v.tensor_scalar(oa, ya, 0.0, HUGE, ALU.is_gt, ALU.mult).then_inc(step, c.inc())
                    v.wait_ge(step, c.now())
                    v.tensor_tensor(oa, oa, la, ALU.add).then_inc(step, c.inc())
                    v.wait_ge(step, c.now())
                    v.nop(nofuse=True)
                    v.copy_predicated(oa, fa, ya).then_inc(step, c.inc())
                    v.wait_ge(step, c.now())
                    v.tensor_tensor(oa, oa, pay[:, r, 0:n, 0:D], ALU.add).then_inc(y_ready, 1)
                    v.engine_nop().then_inc(step, c.inc())
                    assert c.n == PER or is_last(e, i, r), c.n
                units(v, e, unit)
            normalise(0, 0, 0, False, 0)
            SET = 2
            inputs(0, 0, 0, False, 0, Count(0))
            experts(v, expert)

        @block.tensor
        def _(pe):
            pe.wait_ge(consts, 32)
            pe.transpose(ps_T[:, 0, 0:E * KF], b1r[:], ident[0:E * KF, 0:E * KF]).then_inc(b1_turned, 1)
            pe.wait_ge(b1_ready, 1)

            def transposes(n, u, first):
                pe.wait_ge(hn_ready, u + 1)
                if not first:
                    pe.wait_ge(x_ready, u)
                for s in range(n):
                    for k in range(KD):
                        last = pe.transpose(ps_T[:, k, s * P:(s + 1) * P], hn[:, s, k * P:(k + 1) * P], ident[:])
                last.then_inc(turned, 1)

            transposes(SUB, 0, True)

            def expert(e, buf):
                if isinstance(e, int) and e == 0:
                    pe.wait_ge(first_split, 2)
                else:
                    pe.wait_ge(split, e * (2 * UNITS))
                    pe.nop(nofuse=True)

                def unit(i, r, tail):
                    n = subs(r, tail)
                    m = n * P
                    u = e * UNITS + i * RING + r
                    pe.wait_ge(x_ready, u + 1)
                    for f in range(KF):
                        if f >= 2:
                            pe.wait_ge(relu_done, KF * u + f - 1)
                        elif not is_first(e, i, r) or r > 0:
                            pe.wait_ge(relu_done, KF * u + f - 1)
                        passes = [(w, a, k) for k in range(KD) for w, a in ((whi, xhi), (whi, xlo), (wlo, xhi))]
                        for j, (w, a, k) in enumerate(passes):
                            last = pe.matmul(ps_H[:, f % 2, 0:m], w1_at(w, buf, k, f), a[:, k, 0:m],
                                             start=(j == 0), stop=(j == len(passes) - 1))
                        last.then_inc(first_done, 1)
                    if not is_last(e, i, r):
                        nxt = LASTSUB if (r == RING - 2 and isinstance(i, int) and i == ROUNDS - 1) else SUB
                        transposes(nxt, u + 1, False)
                    if not is_first(e, i, r) or r > 0:
                        pe.wait_ge(y_read, u)
                    for f in range(KF):
                        pe.wait_ge(hid_ready, KF * u + f + 1)
                        for s in range(n):
                            cols = slice(s * P, (s + 1) * P)
                            for j, (a, w) in enumerate(((hhi, whi), (hhi, wlo), (hlo, whi))):
                                last = pe.matmul(ps_Y[:, s, 0:D], a[:, f, cols], w2_at(w, buf, f),
                                                 start=(f == 0 and j == 0), stop=(f == KF - 1 and j == 2))
                    last.then_inc(second_done, 1)
                units(pe, e, unit)
            experts(pe, expert)


def build_program(nc, x, src, dst, edge_weight, gate_w, gate_b, w1, b1, w2, b2, out):
    N, D = x.shape
    E = gate_w.shape[1]
    C = max(1, math.ceil(CAPACITY_FACTOR * N / E))
    QUEUE = -(-C // (2 * P)) * (2 * P)
    W = LOGIT + E
    AGG = -(-(N + STEP) // (16 * P)) * (16 * P)
    t = dict(x=x, src=src, dst=dst, weight=edge_weight, gate_w=gate_w, gate_b=gate_b, w1=w1, b1=b1,
             w2=w2, b2=b2, out=out, C=C, QUEUE=QUEUE)
    t["agg"] = nc.dram_tensor("agg", (AGG, D), F16, kind="Internal").ap()
    t["slots"] = nc.dram_tensor("slots", (E * QUEUE, W), F32, kind="Internal").ap()
    with ExitStack() as outer:
        t["ident"] = outer.enter_context(nc.sbuf_tensor("ident", [P, P], F32))
        t["before"] = outer.enter_context(nc.sbuf_tensor("before", [P, P], F16))
        t["ones"] = outer.enter_context(nc.sbuf_tensor("ones", [P, P], F16))
        t["eps"] = outer.enter_context(nc.sbuf_tensor("eps", [P, 1], F32))
        for phase in (edge_and_constants, route_tokens, run_experts):
            with ExitStack() as ctx:
                phase(nc, ctx, t)


_INS = ["x", "src", "dst", "edge_weight", "L0_ffn_gate_w", "L0_ffn_gate_b", "L0_ffn_w1", "L0_ffn_b1",
        "L0_ffn_w2", "L0_ffn_b2"]


def kernel(**inputs):
    import numpy as _np
    import concourse.bacc as _bacc
    from concourse import mybir as _mybir
    from concourse.bass_utils import run_bass_kernel_spmd as _run

    nc = _bacc.Bacc("TRN2", target_bir_lowering=False, num_devices=1)
    arrays, args = {}, []
    for name in _INS:
        a = _np.ascontiguousarray(inputs[name])
        arrays[f"in_{name}"] = a
        args.append(nc.dram_tensor(f"in_{name}", a.shape, _mybir.dt.from_np(a.dtype), kind="ExternalInput").ap())
    out = nc.dram_tensor("out_x", inputs["x"].shape, _mybir.dt.float32, kind="ExternalOutput").ap()
    build_program(nc, *args, out)
    r = _run(nc, [arrays], core_ids=[0])
    return r.results[0]["out_x"]
```

```python
import math
from contextlib import ExitStack

import concourse.bass as bass
from concourse import mybir

ALU = mybir.AluOpType
ACT = mybir.ActivationFunctionType
AX = mybir.AxisListType
F32 = mybir.dt.float32
F32R = mybir.dt.float32r
F16 = mybir.dt.float16
I32 = mybir.dt.int32
U8 = mybir.dt.uint8

P = 128
G = 8
STEP = G * P
EPS = 1e-5
CAPACITY_FACTOR = 1.25
FLAG = float(1 << 20)

MEAN, RSTD, TOKEN, LOGIT = 256, 257, 258, 259
RING = 4


class Count:

    def __init__(self, base):
        self.base, self.n = base, 0

    def inc(self):
        self.n += 1
        return 1

    def now(self):
        return self.base + self.n


def steps(eng, total, unroll, body):
    for r in range(unroll):
        body(0, r)
    with eng.Fori(1, total // unroll) as i:
        for r in range(unroll):
            body(i, r)
    for r in range(total % unroll):
        body(total // unroll, r)


def edge_and_constants(nc, ctx, t):
    x, src, dst, weight = t["x"], t["src"], t["dst"], t["weight"]
    agg = t["agg"]
    N, D = x.shape
    M = src.shape[0]
    S = -(-M // STEP)
    LAST = S - 1
    REPEATED = S * STEP - M
    assert REPEATED < STEP and LAST % 2 == 0

    def base_of(i, r):
        return M - STEP if (isinstance(i, int) and 2 * i + r == LAST) else i * (2 * STEP) + r * STEP

    def sb(name, shape, dt):
        return ctx.enter_context(nc.sbuf_tensor(name, shape, dt))

    def sem(name):
        return ctx.enter_context(nc.semaphore(name))

    zeros = sb("zeros16", [P, 16 * D], F16)
    src_row = sb("src_row", [P, 2, STEP], I32)
    src_col = sb("src_col", [P, 2, G], I32)
    dst_col = sb("dst_col", [P, 2, G], I32)
    w_col = sb("w_col", [P, 2, G], F32)
    w16 = sb("w16", [P, 2, G], F16)
    w32 = sb("w32", [P, 2, G], F32)
    srcf = sb("srcf", [P, 2, G], F32)
    rows = sb("rows", [P, 2, G, D], F32)
    same = sb("same", [P, 2, G, STEP], F16)
    earlier = sb("earlier", [P, 2, G, P], F16)
    stats = sb("e_stats", [P, G, 6], F32)
    mv = sb("e_mv", [P, 2, G, 2], F32)
    std = sb("e_std", [P, 2, G], F32)
    rstd = sb("e_rstd", [P, G], F32)
    msg = sb("msg", [P, 2, G, D], F16)
    norm16 = sb("norm16", [P, G, D], F16)
    sums = sb("sums", [P, 2, G, D], F16)
    spare_i = sb("spare_i", [P, G], I32)
    spare = sb("spare", [P, G], F32)
    shift = sb("shift", [P, G], F32)
    target = sb("target", [P, 2, G], I32)
    ones, before, ident, eps = t["ones"], t["before"], t["ident"], t["eps"]

    ps_sum = ctx.enter_context(nc.psum_tensor("ps_sum", [P, G, D], F32))
    ps_cnt = ctx.enter_context(nc.psum_tensor("ps_cnt", [P, 512], F32))

    set_up = sem("set_up")
    pool_set = sem("pool_set")
    agg_zeroed = sem("agg_zeroed")
    idx_loaded = [sem(f"idx_loaded{r}") for r in range(2)]
    gathered = [sem(f"gathered{r}") for r in range(2)]
    added = [sem(f"added{r}") for r in range(2)]
    masks_ready = sem("masks_ready")
    stats_ready = sem("e_stats_ready")
    std_ready = sem("e_std_ready")
    msg_ready = sem("msg_ready")
    counted = sem("counted")
    summed = sem("summed")
    sums_out = sem("sums_out")
    edge_done = sem("edge_done")
    step = sem("e_step")

    BANKS = G * D // 512
    PER_BANK = G // BANKS
    row_view = lambda ap: ap.rearrange("(p c) -> p c", c=G)
    agg_v = agg.rearrange("(p b r) d -> b p (r d)", p=P, r=16)

    with nc.Block() as block:

        @block.sync
        def _(sp):
            def load(i, r):
                s = 2 * i + r
                if not (isinstance(i, int) and i == 0):
                    sp.wait_ge(edge_done, s - 1)
                b = base_of(i, r)
                sp.dma_start(dst_col[:, r, :], row_view(dst[bass.ds(b, STEP)])).then_inc(idx_loaded[r], 16)
                sp.dma_start(src_col[:, r, :], row_view(src[bass.ds(b, STEP)])).then_inc(idx_loaded[r], 16)
                sp.dma_start(w_col[:, r, :], row_view(weight[bass.ds(b, STEP)])).then_inc(idx_loaded[r], 16)
                sp.dma_start(src_row[:, r, :], src[bass.ds(b, STEP)].partition_broadcast(P))\
                    .then_inc(idx_loaded[r], 16)
            steps(sp, S, 2, load)

        @block.gpsimd
        def _(pool):
            pool.memset(before[:], 1.0).then_inc(pool_set, 1)
            pool.memset(ident[:], 0.0).then_inc(pool_set, 1)
            pool.iota(spare_i[:], [[P, G]], base=N, channel_multiplier=1).then_inc(pool_set, 1)
            pool.wait_ge(pool_set, 3)
            pool.affine_select(out=before[:], in_=before[:], compare_op=ALU.is_gt, fill=0.0, base=0,
                               pattern=[[1, P]], channel_multiplier=-1).then_inc(pool_set, 1)
            pool.affine_select(out=ident[:], in_=ident[:], compare_op=ALU.not_equal, fill=1.0, base=0,
                               pattern=[[-1, P]], channel_multiplier=1).then_inc(pool_set, 1)

            def gather(i, r):
                pool.wait_ge(idx_loaded[r], 64 * (i + 1))
                pool.nop(nofuse=True)
                if not (isinstance(i, int) and i == 0):
                    pool.wait_ge(edge_done, 2 * i + r - 1)
                    pool.nop(nofuse=True)
                for c in range(G):
                    pool.indirect_dma_start(
                        out=rows[:, r, c, :], out_offset=None, in_=x[:, :],
                        in_offset=bass.IndirectOffsetOnAxis(ap=dst_col[:, r, c:c + 1], axis=0),
                    ).then_inc(gathered[r], 16)

            def scatter(i, r):
                s = 2 * i + r
                pool.wait_ge(edge_done, s + 1)
                pool.wait_ge(sums_out, BANKS * (s + 1))
                pool.nop(nofuse=True)
                if isinstance(i, int) and s == 0:
                    pool.wait_ge(agg_zeroed, 16 * agg_v.shape[0])
                else:
                    pool.wait_ge(added[1 - r], 16 * G * (i + r))
                    pool.nop(nofuse=True)
                for c in range(G):
                    pool.indirect_dma_start(
                        out=agg[:, :], out_offset=bass.IndirectOffsetOnAxis(ap=target[:, r, c:c + 1], axis=0),
                        in_=sums[:, r, c, :], in_offset=None, compute_op=ALU.add,
                    ).then_inc(added[r], 16)

            gather(0, 0)
            gather(0, 1)
            scatter(0, 0)
            gather(1, 0)
            scatter(0, 1)
            with pool.Fori(1, S // 2) as i:
                gather(i, 1)
                scatter(i, 0)
                gather(i + 1, 0)
                scatter(i, 1)
            scatter(S // 2, 0)
            pool.wait_ge(added[0], 16 * G * (S // 2 + 1))
            pool.wait_ge(added[1], 16 * G * (S // 2))

        @block.scalar
        def _(act):
            act.wait_ge(set_up, 2)
            with act.Fori(0, agg_v.shape[0]) as b:
                act.dma_start(agg_v[b], zeros[:]).then_inc(agg_zeroed, 16)

            def body(i, r):
                s = 2 * i + r
                act.wait_ge(stats_ready, s + 1)
                act.activation(std[:, r, :], mv[:, r, :, 1], ACT.Sqrt, bias=eps[:, 0:1]).then_inc(std_ready, 1)
                if not (isinstance(i, int) and i == 0):
                    act.wait_ge(added[r], 16 * G * i)
                for b in range(BANKS):
                    act.wait_ge(summed, BANKS * s + b + 1)
                    part = slice(b * PER_BANK, (b + 1) * PER_BANK)
                    act.activation(sums[:, r, part, :], ps_sum[:, part, :], ACT.Copy).then_inc(sums_out, 1)
            steps(act, S, 2, body)

        @block.vector
        def _(v):
            v.memset(zeros[:], 0.0).then_inc(set_up, 1)
            v.memset(eps[:], EPS).then_inc(set_up, 1)
            v.memset(ones[:], 1.0)
            v.wait_ge(pool_set, 5)
            v.tensor_copy(spare[:], spare_i[:]).then_inc(step, 1)
            v.wait_ge(step, 1)
            SET, PER = 1, 8

            def body(i, r):
                s = 2 * i + r
                n = Count(s * PER + SET)
                v.wait_ge(idx_loaded[r], 64 * (i + 1))
                v.tensor_copy(srcf[:, r, :], src_col[:, r, :])
                v.tensor_copy(w16[:, r, :], w_col[:, r, :]).then_inc(step, n.inc())
                v.wait_ge(step, n.now())
                v.tensor_copy(w32[:, r, :], w16[:, r, :]).then_inc(step, n.inc())
                if isinstance(i, int) and s == LAST and REPEATED:
                    assert REPEATED % G == 0
                    v.wait_ge(step, n.now())
                    v.memset(w32[0:REPEATED // G, r, :], 0.0).then_inc(step, 1)
                    n.base += 1
                if not (isinstance(i, int) and i == 0):
                    v.wait_ge(summed, BANKS * (s - 1))
                for c in range(G):
                    last = v.tensor_scalar(same[:, r, c, :], src_row[:, r, :], srcf[:, r, c:c + 1], None,
                                           ALU.is_equal)
                last.then_inc(step, n.inc())
                v.wait_ge(step, n.now())
                for c in range(G):
                    last = v.tensor_tensor(earlier[:, r, c, :],
                                           same[:, r, c, :].rearrange("j (p a) -> j a p", a=G)[:, c, :],
                                           before[:], ALU.mult)
                last.then_inc(masks_ready, 1)
                v.wait_ge(gathered[r], 16 * G * (i + 1))
                for c in range(G):
                    last = v.bn_stats(stats[:, c, :], rows[:, r, c, :])
                last.then_inc(step, n.inc())
                v.wait_ge(step, n.now())
                v.nop(nofuse=True)
                for c in range(G):
                    last = v.bn_aggr(mv[:, r, c, :], stats[:, c, :])
                last.then_inc(stats_ready, 1)
                v.tensor_tensor(shift[:], spare[:], srcf[:, r, :], ALU.subtract).then_inc(step, n.inc())
                v.wait_ge(std_ready, s + 1)
                v.reciprocal(rstd[:], std[:, r, :]).then_inc(step, n.inc())
                v.wait_ge(step, n.now())
                for c in range(G):
                    last = v.tensor_scalar(norm16[:, c, :], rows[:, r, c, :], mv[:, r, c, 0:1], rstd[:, c:c + 1],
                                           ALU.subtract, ALU.mult)
                last.then_inc(step, n.inc())
                v.wait_ge(step, n.now())
                for c in range(G):
                    last = v.tensor_scalar(msg[:, r, c, :], norm16[:, c, :], w32[:, r, c:c + 1], None, ALU.mult)
                last.then_inc(msg_ready, 1)
                v.wait_ge(counted, s + 1)
                v.scalar_tensor_tensor(out=shift[:], in0=ps_cnt[:, 0:G], scalar=0.5, in1=shift[:],
                                       op0=ALU.is_gt, op1=ALU.mult).then_inc(step, n.inc())
                v.wait_ge(step, n.now())
                if not (isinstance(i, int) and i == 0):
                    v.wait_ge(added[r], 16 * G * i)
                v.tensor_tensor(target[:, r, :], shift[:], srcf[:, r, :], ALU.add).then_inc(edge_done, 1)
                assert n.n == PER, n.n
            steps(v, S, 2, body)

        @block.tensor
        def _(pe):
            def body(i, r):
                s = 2 * i + r
                seen = lambda b, c: same[:, r, b, :].rearrange("j (p a) -> j a p", a=G)[:, c, :]
                pe.wait_ge(masks_ready, s + 1)
                if not (isinstance(i, int) and s == 0):
                    pe.wait_ge(edge_done, s)
                for c in range(G):
                    for b in range(c):
                        pe.matmul(ps_cnt[:, c:c + 1], seen(b, c), ones[:, 0:1], start=(b == 0), stop=False)
                    last = pe.matmul(ps_cnt[:, c:c + 1], earlier[:, r, c, :], ones[:, 0:1],
                                     start=(c == 0), stop=True)
                last.then_inc(counted, 1)
                pe.wait_ge(msg_ready, s + 1)
                for k in range(BANKS):
                    if not (isinstance(i, int) and s == 0):
                        pe.wait_ge(sums_out, BANKS * (s - 1) + k + 1)
                    for c in range(k * PER_BANK, (k + 1) * PER_BANK):
                        for b in range(G):
                            last = pe.matmul(ps_sum[:, c, :], seen(b, c), msg[:, r, b, :],
                                             start=(b == 0), stop=(b == G - 1))
                    last.then_inc(summed, 1)
            steps(pe, S, 2, body)


def route_tokens(nc, ctx, t):
    x, agg, slots, out = t["x"], t["agg"], t["slots"], t["out"]
    gate_w, gate_b = t["gate_w"], t["gate_b"]
    N, D = x.shape
    E = gate_w.shape[1]
    KD = D // P
    W = slots.shape[1]
    C, QUEUE = t["C"], t["QUEUE"]
    S = -(-N // STEP)
    LAST = S - 1
    REPEATED = S * STEP - N
    assert LAST % RING == 0

    def base_of(i, r):
        s = RING * i + r
        return N - STEP if (isinstance(i, int) and s == LAST) else i * (RING * STEP) + r * STEP

    def sb(name, shape, dt):
        return ctx.enter_context(nc.sbuf_tensor(name, shape, dt))

    def sem(name):
        return ctx.enter_context(nc.semaphore(name))

    xt = sb("xt", [P, 2, G, D], F32)
    at = sb("at", [P, 2, G, D], F16)
    pay = sb("pay", [P, RING, G, W], F32)
    h = sb("h", [P, 2, G, D], F32)
    hT = sb("hT", [P, G * KD, P], F32)
    gw = sb("gw", [P, KD, E], F32)
    gb = sb("gb", [P, E], F32)
    stats = sb("t_stats", [P, G, 6], F32)
    mv = sb("t_mv", [P, 2, G, 2], F32)
    std = sb("t_std", [P, 2, G], F32)
    shift = sb("t_shift", [P, 2, G], F32)
    token_i = sb("token_i", [P, G], I32)
    token = sb("token", [P, G], F32)
    expert_i = sb("expert_i", [P, E], I32)
    expert = sb("expert", [P, E], F32)
    prefer = sb("prefer", [P, E], F32)
    limit = sb("limit", [P, E], F32)
    fresh = sb("fresh", [P, G], F16)
    lg = sb("lg", [P, G, E], F32)
    cand = sb("cand", [P, G, E], F32)
    top = sb("top", [P, G], F32)
    best = sb("best", [P, G], F32)
    hot = sb("hot", [P, 2, G, E], F16)
    place = sb("place", [P, 2, G + 1, E], F32)
    kept_hot = sb("kept_hot", [P, G, E], F32)
    own = sb("own", [P, G, E], F32)
    kept = sb("kept", [P, G], F32)
    where = sb("where", [P, G], F32)
    slot_i = sb("slot_i", [P, RING, G], I32)
    ones, before, ident, eps = t["ones"], t["before"], t["ident"], t["eps"]

    ps_T = ctx.enter_context(nc.psum_tensor("ps_T", [P, G * KD, P], F32))
    ps_L = ctx.enter_context(nc.psum_tensor("ps_L", [P, 512], F32))
    ps_R = ctx.enter_context(nc.psum_tensor("ps_R", [P, 512], F32))
    logits = ps_L[:, 0:G * E].rearrange("p (g e) -> p g e", g=G)
    ranks = ps_R[:, 0:(G + 1) * E].rearrange("p (g e) -> p g e", g=G + 1)

    bound_i = sb("bound_i", [1, E, t["UMAX"]], I32)
    filled = sb("filled", [1, E], F32)
    queued = sb("queued", [1, E], F32)
    over = sb("over", [1, E, t["UMAX"]], F32)
    count = sb("count", [1, E], F32)
    begin = sb("begin", [1, E + 1], F32)
    offset = sb("offset", [1, E], F32)
    first_unit, first_row, first_blank = t["first_unit"], t["first_row"], t["first_blank"]

    consts = sem("t_consts")
    pool_set = sem("t_pool_set")
    loaded = [sem(f"t_loaded{r}") for r in range(2)]
    x1_ready = sem("x1_ready")
    stats_ready = sem("t_stats_ready")
    std_ready = sem("t_std_ready")
    norm_ready = sem("norm_ready")
    h_ready = sem("h_ready")
    turned = sem("turned")
    hT_ready = sem("hT_ready")
    gated = sem("gated")
    hot_ready = sem("hot_ready")
    ranked = sem("ranked")
    slot_ready = sem("slot_ready")
    out_written = [sem(f"out_written{r}") for r in range(RING)]
    sent = [sem(f"sent{r}") for r in range(RING)]
    step = sem("t_step")
    step_b = sem("t_step_b")

    BANKS = G * KD * P // 512
    PER_BANK = G * KD // BANKS

    with nc.Block() as block:

        @block.sync
        def _(sp):
            sp.dma_start(gw[:], gate_w.rearrange("(k p) e -> p k e", p=P)).then_inc(consts, 16)
            sp.dma_start(gb[:], gate_b.partition_broadcast(P)).then_inc(consts, 16)

            def load(i, r):
                s = RING * i + r
                if not (isinstance(i, int) and s < 2):
                    sp.wait_ge(x1_ready, s - 1)
                b = base_of(i, r)
                sp.dma_start(xt[:, r % 2], x[bass.ds(b, STEP), :].rearrange("(g p) d -> p g d", p=P))\
                    .then_inc(loaded[r % 2], 16)
                sp.dma_start(at[:, r % 2], agg[bass.ds(b, STEP), :].rearrange("(g p) d -> p g d", p=P))\
                    .then_inc(loaded[r % 2], 16)

            def store(i, r, b):
                sp.wait_ge(x1_ready, RING * i + r + 1)
                sp.dma_start(out[bass.ds(b, STEP), :].rearrange("(g p) d -> p g d", p=P), pay[:, r, :, 0:D])\
                    .then_inc(out_written[r], 16)

            load(0, 0)
            for r in range(1, RING):
                load(0, r)
                store(0, r - 1, base_of(0, r - 1))
            with sp.Fori(1, S // RING) as i:
                for r in range(RING):
                    load(i, r)
                    if r:
                        store(i, r - 1, base_of(i, r - 1))
                    else:
                        store(i - 1, RING - 1, base_of(i - 1, RING - 1))
            n = S // RING
            load(n, 0)
            store(n - 1, RING - 1, base_of(n - 1, RING - 1))
            sp.wait_ge(out_written[RING - 1], 16 * n)
            store(n, 0, base_of(n, 0))
            for r in range(RING):
                sp.wait_ge(out_written[r], 16 * (n + (r == 0)))

        @block.gpsimd
        def _(pool):
            pool.iota(token_i[:], [[P, G]], base=0, channel_multiplier=1).then_inc(pool_set, 1)
            pool.iota(expert_i[:], [[1, E]], base=0, channel_multiplier=0).then_inc(pool_set, 1)
            pool.iota(bound_i[:], [[0, E], [t["UNIT"], t["UMAX"]]], base=0, channel_multiplier=0)\
                .then_inc(pool_set, 1)
            pool.memset(fresh[:], 1.0).then_inc(pool_set, 1)
            pool.wait_ge(pool_set, 4)
            pool.affine_select(out=fresh[:], in_=fresh[:], compare_op=ALU.is_ge, fill=0.0, base=-REPEATED,
                               pattern=[[P, G]], channel_multiplier=1).then_inc(pool_set, 1)

            def body(i, r):
                pool.wait_ge(slot_ready, RING * i + r + 1)
                pool.nop(nofuse=True)
                for g in range(G):
                    pool.indirect_dma_start(
                        out=slots[:, :], out_offset=bass.IndirectOffsetOnAxis(ap=slot_i[:, r, g:g + 1], axis=0),
                        in_=pay[:, r, g, :], in_offset=None, bounds_check=E * QUEUE - 1, oob_is_err=False,
                    ).then_inc(sent[r], 16)
            steps(pool, S, RING, body)
            for r in range(RING):
                pool.wait_ge(sent[r], 16 * G * (S // RING + (r < S % RING)))

        @block.scalar
        def _(act):
            def body(i, r):
                s = RING * i + r
                q = r % 2
                act.wait_ge(stats_ready, s + 1)
                act.activation(std[:, q, :], mv[:, q, :, 1], ACT.Sqrt, bias=eps[:, 0:1]).then_inc(std_ready, 1)
                act.wait_ge(norm_ready, s + 1)
                if not (isinstance(i, int) and s < 2):
                    act.wait_ge(turned, BANKS * (s - 1))
                if not (isinstance(i, int) and s < 1):
                    act.wait_ge(gated, s)
                act.nop(nofuse=True)

                def copy(k):
                    act.wait_ge(turned, BANKS * s + k + 1)
                    part = slice(k * PER_BANK, (k + 1) * PER_BANK)
                    act.activation(hT[:, part, :], ps_T[:, part, :], ACT.Copy).then_inc(hT_ready, 1)

                for k in range(BANKS):
                    for g in range(k * G // BANKS, (k + 1) * G // BANKS):
                        last = act.activation(h[:, q, g, :], pay[:, r, g, 0:D], ACT.Identity,
                                              bias=shift[:, q, g:g + 1], scale=pay[:, r, g, RSTD:RSTD + 1])
                    last.then_inc(h_ready, 1)
                    if k:
                        copy(k - 1)
                copy(BANKS - 1)
            steps(act, S, RING, body)

        @block.tensor
        def _(pe):
            def rank(i, r):
                s = RING * i + r
                q = r % 2
                pe.wait_ge(hot_ready, s + 1)
                if not (isinstance(i, int) and s < 1):
                    pe.wait_ge(slot_ready, s)
                pe.matmul(ranks[:, 0:G, :], before[:], hot[:, q], start=True, stop=False, skip_group_check=True)
                for g in range(G):
                    last = pe.matmul(ranks[:, g + 1:G + 1, :], ones[:],
                                     hot[:, q, g, :].unsqueeze(1).broadcast_to([P, G - g, E]),
                                     start=False, stop=(g == G - 1), skip_group_check=True)
                last.then_inc(ranked, 1)

            def gate(s, k, i):
                pe.wait_ge(hT_ready, BANKS * s + k + 1)
                if not (isinstance(i, int) and isinstance(s, int) and s < 1):
                    pe.wait_ge(hot_ready, s)
                else:
                    pe.wait_ge(consts, 32)
                for g in range(k * G // BANKS, (k + 1) * G // BANKS):
                    for kd in range(KD):
                        last = pe.matmul(logits[:, g, :], hT[:, g * KD + kd, :], gw[:, kd, :],
                                         start=(kd == 0), stop=(kd == KD - 1))
                if k == BANKS - 1:
                    last.then_inc(gated, 1)

            def body(i, r):
                s = RING * i + r
                q = r % 2
                if not (isinstance(i, int) and s < 1):
                    rank(*((i, r - 1) if r else (i - 1, RING - 1)))
                for k in range(BANKS):
                    pe.wait_ge(h_ready, BANKS * s + k + 1)
                    if not (isinstance(i, int) and s < 1):
                        pe.wait_ge(hT_ready, BANKS * (s - 1) + k + 1)
                    for n in range(k * PER_BANK, (k + 1) * PER_BANK):
                        g, kd = divmod(n, KD)
                        last = pe.transpose(ps_T[:, n, :], h[:, q, g, kd * P:(kd + 1) * P], ident[:])
                    last.then_inc(turned, 1)
                    if k:
                        gate(s, k - 1, i)
                gate(s, BANKS - 1, i)
            steps(pe, S, RING, body)
            rank(LAST // RING, 0)

        @block.vector
        def _(v):
            v.wait_ge(pool_set, 5)
            v.tensor_copy(token[:], token_i[:])
            v.tensor_copy(expert[:], expert_i[:]).then_inc(step, 1)
            v.wait_ge(step, 1)
            v.tensor_scalar(prefer[:], expert[:], -1.0, float(E), ALU.mult, ALU.add)
            v.tensor_scalar(limit[:], expert[:], float(QUEUE), float(C), ALU.mult, ALU.add)
            v.tensor_scalar(place[:, 1, G, :], expert[:], float(QUEUE), None, ALU.mult).then_inc(step, 1)
            v.wait_ge(step, 2)
            v.wait_ge(consts, 32)
            SET, PER_A, PER_B = 2, 4, 12

            def statistics(i, r, n):
                s = RING * i + r
                q = r % 2
                last_step = isinstance(i, int) and s == LAST
                v.wait_ge(loaded[q], 32 * ((RING // 2) * i + r // 2 + 1))
                if not (isinstance(i, int) and i == 0):
                    v.wait_ge(sent[r], 16 * G * i)
                    v.wait_ge(out_written[r], 16 * i)
                v.tensor_tensor(pay[:, r, :, 0:D], xt[:, q], at[:, q], ALU.add).then_inc(x1_ready, 1)
                v.wait_ge(x1_ready, s + 1)
                for g in range(G):
                    last = v.bn_stats(stats[:, g, :], pay[:, r, g, 0:D])
                last.then_inc(step, n.inc())
                if last_step:
                    v.tensor_scalar(token[:], token[:], -float(REPEATED), None, ALU.add).then_inc(step, n.inc())
                else:
                    v.engine_nop().then_inc(step, n.inc())
                v.wait_ge(step, n.now())
                v.nop(nofuse=True)
                for g in range(G):
                    last = v.bn_aggr(mv[:, q, g, :], stats[:, g, :])
                last.then_inc(stats_ready, 1)

            def scales(i, r, n):
                s = RING * i + r
                q = r % 2
                v.tensor_copy(pay[:, r, :, TOKEN].bitcast(I32), token[:]).then_inc(step, n.inc())
                v.wait_ge(step, n.now())
                v.tensor_scalar(token[:], token[:], float(STEP), None, ALU.add)
                v.tensor_copy(pay[:, r, :, MEAN], mv[:, q, :, 0])
                v.wait_ge(std_ready, s + 1)
                v.reciprocal(pay[:, r, :, RSTD], std[:, q, :]).then_inc(step, n.inc())
                v.wait_ge(step, n.now())
                v.scalar_tensor_tensor(out=shift[:, q, :], in0=mv[:, q, :, 0], scalar=-1.0,
                                       in1=pay[:, r, :, RSTD], op0=ALU.mult, op1=ALU.mult)\
                    .then_inc(norm_ready, 1)
                assert n.n == PER_A, n.n

            def choice(i, r, n):
                s = RING * i + r
                q = r % 2
                last_step = isinstance(i, int) and s == LAST
                v.wait_ge(gated, s + 1)
                v.tensor_tensor(lg[:], logits, gb[:].unsqueeze(1).broadcast_to([P, G, E]), ALU.add)\
                    .then_inc(step_b, n.inc())
                v.wait_ge(step_b, n.now())
                v.tensor_reduce(top[:], lg[:], AX.X, ALU.max).then_inc(step_b, n.inc())
                v.wait_ge(step_b, n.now())
                less = pay[:, r, :, LOGIT:LOGIT + E]
                v.tensor_tensor(less, lg[:], top[:].unsqueeze(2).broadcast_to([P, G, E]), ALU.subtract)\
                    .then_inc(step_b, n.inc())
                v.wait_ge(step_b, n.now())
                v.scalar_tensor_tensor(out=cand[:], in0=less, scalar=0.0,
                                       in1=prefer[:].unsqueeze(1).broadcast_to([P, G, E]),
                                       op0=ALU.is_equal, op1=ALU.mult).then_inc(step_b, n.inc())
                v.wait_ge(step_b, n.now())
                v.tensor_reduce(best[:], cand[:], AX.X, ALU.max).then_inc(step_b, n.inc())
                v.wait_ge(step_b, n.now())
                if last_step:
                    v.tensor_tensor(own[:], cand[:], best[:].unsqueeze(2).broadcast_to([P, G, E]), ALU.is_equal)\
                        .then_inc(step_b, n.inc())
                    v.wait_ge(step_b, n.now())
                    v.tensor_tensor(hot[:, q], own[:], fresh[:].unsqueeze(2).broadcast_to([P, G, E]), ALU.mult)\
                        .then_inc(hot_ready, 1)
                else:
                    v.tensor_tensor(hot[:, q], cand[:], best[:].unsqueeze(2).broadcast_to([P, G, E]), ALU.is_equal)\
                        .then_inc(hot_ready, 1)
                    v.engine_nop().then_inc(step_b, n.inc())

            def slot(i, r, n):
                s = RING * i + r
                q = r % 2
                v.wait_ge(ranked, s + 1)
                v.wait_ge(hot_ready, s + 1)
                v.tensor_tensor(place[:, q], ranks, place[:, 1 - q, G, :].unsqueeze(1).broadcast_to([P, G + 1, E]),
                                ALU.add).then_inc(step_b, n.inc())
                v.wait_ge(step_b, n.now())
                v.tensor_tensor(kept_hot[:], place[:, q, 0:G, :], limit[:].unsqueeze(1).broadcast_to([P, G, E]),
                                ALU.is_lt)
                v.tensor_tensor(own[:], place[:, q, 0:G, :], hot[:, q], ALU.mult).then_inc(step_b, n.inc())
                v.wait_ge(step_b, n.now())
                v.tensor_tensor(kept_hot[:], kept_hot[:], hot[:, q], ALU.mult).then_inc(step_b, n.inc())
                v.tensor_reduce(where[:], own[:], AX.X, ALU.add).then_inc(step_b, n.inc())
                v.wait_ge(step_b, n.now())
                v.tensor_reduce(kept[:], kept_hot[:], AX.X, ALU.add).then_inc(step_b, n.inc())
                v.wait_ge(step_b, n.now())
                v.scalar_tensor_tensor(out=where[:], in0=kept[:], scalar=-FLAG, in1=where[:],
                                       op0=ALU.mult, op1=ALU.add).then_inc(step_b, n.inc())
                v.wait_ge(step_b, n.now())
                v.tensor_scalar(slot_i[:, r, :], where[:], FLAG, None, ALU.add).then_inc(slot_ready, 1)
                assert n.n == PER_B, n.n

            def body(i, r):
                s = RING * i + r
                a, b = Count(s * PER_A + SET), Count((s - 1) * PER_B)
                before_it = (i, r - 1) if r else (i - 1, RING - 1)
                statistics(i, r, a)
                scales(i, r, a)
                if not (isinstance(i, int) and s == 0):
                    choice(*before_it, b)
                    slot(*before_it, b)
            steps(v, S, RING, body)
            b = Count(LAST * PER_B)
            choice(LAST // RING, 0, b)
            slot(LAST // RING, 0, b)
            n = Count(S * PER_A + SET)
            v.wait_ge(slot_ready, S)
            v.tensor_tensor(filled[:], place[0:1, LAST % 2, G, :], limit[0:1, :], ALU.min).then_inc(step, n.inc())
            v.wait_ge(step, n.now())
            v.scalar_tensor_tensor(out=queued[:], in0=expert[0:1, :], scalar=-float(QUEUE), in1=filled[:],
                                   op0=ALU.mult, op1=ALU.add).then_inc(step, n.inc())
            v.wait_ge(step, n.now())
            v.tensor_tensor(over[:], queued[:].unsqueeze(2).broadcast_to([1, E, t["UMAX"]]), bound_i[:], ALU.is_gt)\
                .then_inc(step, n.inc())
            v.wait_ge(step, n.now())
            v.tensor_reduce(count[:], over[:], AX.X, ALU.add).then_inc(step, n.inc())
            v.memset(begin[:], 0.0).then_inc(step, n.inc())
            v.wait_ge(step, n.now())
            for e in range(E):
                v.scalar_tensor_tensor(out=begin[:, e + 1:e + 2], in0=count[:, e:e + 1], scalar=1.0,
                                       in1=begin[:, e:e + 1], op0=ALU.max, op1=ALU.add).then_inc(step, n.inc())
                v.wait_ge(step, n.now())
            v.tensor_scalar(offset[:], expert[0:1, :], float(QUEUE), None, ALU.mult).then_inc(step, n.inc())
            v.wait_ge(step, n.now())
            v.scalar_tensor_tensor(out=offset[:], in0=begin[:, 0:E], scalar=-float(t["UNIT"]), in1=offset[:],
                                   op0=ALU.mult, op1=ALU.add).then_inc(step, n.inc())
            v.wait_ge(step, n.now())
            v.tensor_copy(first_unit[:], begin[:])
            v.tensor_copy(first_row[:], offset[:])
            v.tensor_copy(first_blank[:], filled[:]).then_inc(step, n.inc())


def run_experts(nc, ctx, t):
    slots, out = t["slots"], t["out"]
    w1, b1, w2, b2 = t["w1"], t["b1"], t["w2"], t["b2"]
    first_unit, first_row, first_blank = t["first_unit"], t["first_row"], t["first_blank"]
    E, D, F = w1.shape
    N = out.shape[0]
    W = slots.shape[1]
    QUEUE, UNIT, UMAX = t["QUEUE"], t["UNIT"], t["UMAX"]
    KD, KF = D // P, F // P
    SUB = UNIT // P
    WF = KD * F
    assert KF * D == WF and E >= 6 and E % 2 == 0
    HUGE = 1e4

    def sb(name, shape, dt):
        return ctx.enter_context(nc.sbuf_tensor(name, shape, dt))

    def sem(name):
        return ctx.enter_context(nc.semaphore(name))

    raw = sb("raw", [P, 2 * WF], F32)
    whi = sb("whi", [P, 2, 2 * WF], F32R)
    wlo = sb("wlo", [P, 2, 2 * WF], F32R)
    b1r = sb("b1r", [E * KF, P], F32)
    b1c = sb("b1c", [P, E * KF], F32)
    b1e = sb("b1e", [P, KF], F32)
    b2b = sb("b2b", [P, E, D], F32)
    b2e = sb("b2e", [P, D], F32)
    pay = sb("u_pay", [P, RING, SUB, W], F32)
    scales = sb("scales", [P, SUB, 2], F32)
    token = sb("u_token", [P, SUB], I32)
    hn = sb("hn", [P, SUB, D], F32)
    xhi = sb("xhi", [P, KD, UNIT], F32R)
    xlo = sb("xlo", [P, KD, UNIT], F32R)
    hm = sb("hm", [P, KF, UNIT], F32)
    hhi = sb("hhi", [P, KF, UNIT], F32R)
    hlo = sb("hlo", [P, KF, UNIT], F32R)
    ex = sb("ex", [P, SUB, E], F32)
    total = sb("total", [P, SUB], F32)
    prob = sb("prob", [P, SUB], F32)
    y = sb("y", [P, SUB, D], F32)
    low = sb("low", [P, SUB, D], F32)
    finite = sb("finite", [P, SUB, D], U8)
    yo = sb("yo", [P, SUB, D], F32)
    ident = t["ident"]

    ps_T = ctx.enter_context(nc.psum_tensor("u_T", [P, KD, UNIT], F32))
    ps_H = ctx.enter_context(nc.psum_tensor("u_H", [P, 2, UNIT], F32))
    ps_Y = ctx.enter_context(nc.psum_tensor("u_Y", [P, SUB, 512], F32))

    consts = sem("u_consts")
    blank_set = sem("blank_set")
    blanked = sem("blanked")
    b1_turned = sem("b1_turned")
    b1_ready = sem("b1_ready")
    b1_own = sem("b1_own")
    b2_own = sem("b2_own")
    first_loaded = sem("first_loaded")
    raw_loaded = sem("raw_loaded")
    split = sem("split")
    pay_loaded = sem("pay_loaded")
    y_sent = sem("y_sent")
    y_clear = sem("y_clear")
    hn_ready = sem("hn_ready")
    ex_ready = sem("ex_ready")
    prob_ready = sem("prob_ready")
    turned = sem("u_turned")
    xhi_ready = sem("xhi_ready")
    x_ready = sem("x_ready")
    first_done = sem("first_done")
    relu_done = sem("relu_done")
    hhi_ready = sem("hhi_ready")
    hid_ready = sem("hid_ready")
    second_done = sem("second_done")
    y_read = sem("y_read")
    y_ready = sem("y_ready")
    scales_ready = sem("scales_ready")
    step = sem("u_step")
    SEED = dict(y_clear=1, prob_ready=1, relu_done=2, hid_ready=KF, y_read=1, y_ready=RING)

    w1_at = lambda w, b, k, f: w[:, b, k * F + f * P:k * F + (f + 1) * P]
    w2_at = lambda w, b, f: w[:, b, WF + f * D:WF + (f + 1) * D]

    def experts(eng, body):
        def one(e, buf):
            begin = eng.value_load(first_unit[0:1, bass.ds(e, 1)], min_val=0, max_val=(E - 1) * UMAX)
            end = eng.value_load(first_unit[0:1, bass.ds(e + 1, 1)], min_val=1, max_val=E * UMAX)
            body(e, buf, begin, end)
        one(0, 0)
        with eng.Fori(0, (E - 4) // 2) as q:
            one(2 * q + 1, 1)
            one(2 * q + 2, 0)
        for e in range(E - 3, E):
            one(e, e % 2)

    with nc.Block() as block:

        @block.sync
        def _(sp):
            sp.dma_start(b1r[:], b1.rearrange("e (k p) -> (e k) p", p=P)).then_inc(consts, 16)
            sp.dma_start(b2b[:], b2.partition_broadcast(P)).then_inc(consts, 16)
            sp.wait_ge(blank_set, 2)
            for e in range(E):
                row = sp.value_load(first_blank[0:1, e:e + 1], min_val=e * QUEUE, max_val=(e + 1) * QUEUE - UNIT)
                sp.dma_start(slots[bass.ds(row, UNIT), :].rearrange("(s p) w -> p s w", p=P),
                             pay[:, RING - 1, :, :]).then_inc(blanked, 16)
            sp.wait_ge(blanked, 16 * E)

            def load(u, row):
                sp.dma_start(pay[:, u % RING, :, :], slots[bass.ds(row, UNIT), :].rearrange("(s p) w -> p s w", p=P))\
                    .then_inc(pay_loaded, 16)

            def expert(e, buf, begin, end):
                at = sp.value_load(first_row[0:1, bass.ds(e, 1)], min_val=0, max_val=E * QUEUE - UNIT)
                with sp.Fori(begin, end) as u:
                    sp.wait_ge(y_ready, u + (1 - RING + SEED["y_ready"]))
                    sp.nop(nofuse=True)
                    load(u, (u * UNIT + at).with_bounds(min_val=0, max_val=E * QUEUE - UNIT))
                    sp.wait_ge(pay_loaded, 16 * (u + 1))
                    sp.nop(nofuse=True)
            experts(sp, expert)
            units = sp.value_load(first_unit[0:1, E:E + 1], min_val=E, max_val=E * UMAX)
            sp.wait_ge(y_ready, units + (1 - RING + SEED["y_ready"]))
            sp.nop(nofuse=True)
            load(units, 0)
            sp.wait_ge(pay_loaded, 16 * (units + 1))
            sp.nop(nofuse=True)

        @block.gpsimd
        def _(pool):
            def load_weights(e):
                pool.dma_start(raw[:, 0:WF].rearrange("p (k f) -> p k f", k=KD),
                               w1[bass.ds(e, 1)].rearrange("o (k p) f -> (o p) k f", p=P)).then_inc(raw_loaded, 16)
                pool.dma_start(raw[:, WF:2 * WF].rearrange("p (k d) -> p k d", k=KF),
                               w2[bass.ds(e, 1)].rearrange("o (k p) d -> (o p) k d", p=P)).then_inc(raw_loaded, 16)

            def split_weights(e, buf):
                pool.wait_ge(raw_loaded, 32 * e)
                pool.nop(nofuse=True)
                pool.tensor_copy(whi[:, buf, :], raw[:]).then_inc(split, 1)
                pool.wait_ge(split, 2 * e + 1)
                pool.tensor_tensor(wlo[:, buf, :], raw[:], whi[:, buf, :].bitcast(F32), ALU.subtract)\
                    .then_inc(split, 1)

            pool.sem_inc(y_clear, SEED["y_clear"])
            pool.wait_ge(split, 2)
            load_weights(1)

            def expert(e, buf, begin, end):
                if not (isinstance(e, int) and e == E - 1):
                    split_weights(e + 1, 1 - buf)
                if not (isinstance(e, int) and e >= E - 2):
                    pool.wait_ge(split, 2 * (e + 2))
                    pool.nop(nofuse=True)
                    load_weights(e + 2)
                with pool.Fori(begin, end) as u:
                    pool.wait_ge(y_ready, u + 1 + SEED["y_ready"])
                    pool.nop(nofuse=True)
                    for s in range(SUB):
                        pool.indirect_dma_start(
                            out=out[:, :], out_offset=bass.IndirectOffsetOnAxis(ap=token[:, s:s + 1], axis=0),
                            in_=yo[:, s, :], in_offset=None, bounds_check=N - 1, oob_is_err=False,
                        ).then_inc(y_sent, 16)
                    pool.wait_ge(y_sent, 16 * SUB * (u + 1))
                    pool.nop(nofuse=True)
                    pool.sem_inc(y_clear, 1)
            experts(pool, expert)

        @block.scalar
        def _(act):
            act.dma_start(raw[:, 0:WF].rearrange("p (k f) -> p k f", k=KD),
                          w1[0].rearrange("(k p) f -> p k f", p=P)).then_inc(first_loaded, 16)
            act.dma_start(raw[:, WF:2 * WF].rearrange("p (k d) -> p k d", k=KF),
                          w2[0].rearrange("(k p) d -> p k d", p=P)).then_inc(first_loaded, 16)
            act.sem_inc(relu_done, SEED["relu_done"])

            def upper(u):
                act.wait_ge(turned, u + 1)
                act.activation(xhi[:], ps_T[:], ACT.Copy).then_inc(xhi_ready, 1)

            def expert(e, buf, begin, end):
                act.activation(b1e[:], b1c[:, bass.ds(e * KF, KF)], ACT.Copy).then_inc(b1_own, 1)
                act.wait_ge(b1_own, e + 1)
                act.nop(nofuse=True)
                with act.Fori(begin, end) as u:
                    act.wait_ge(hn_ready, u + 1)
                    act.wait_ge(prob_ready, u + SEED["prob_ready"])
                    act.nop(nofuse=True)
                    act.activation(ex[:], pay[:, u % RING, :, LOGIT:LOGIT + E], ACT.Exp).then_inc(ex_ready, 1)
                    for f in range(KF):
                        act.wait_ge(first_done, KF * u + (f + 1))
                        act.wait_ge(hid_ready, KF * u + (f + 1 - KF + SEED["hid_ready"]))
                        act.activation(hm[:, f, :], ps_H[:, f % 2, :], ACT.Relu, bias=b1e[:, f:f + 1])\
                            .then_inc(relu_done, 1)
                        act.wait_ge(relu_done, KF * u + (f + 1 + SEED["relu_done"]))
                        act.activation(hhi[:, f, :], hm[:, f, :], ACT.Copy).then_inc(hhi_ready, 1)
                    upper(u + 1)
            act.wait_ge(b1_ready, 1)
            upper(0)
            experts(act, expert)

        @block.vector
        def _(v):
            blank = pay[:, RING - 1, :, :]
            v.memset(blank, 0.0).then_inc(blank_set, 1)
            v.wait_ge(blank_set, 1)
            v.memset(blank[:, :, TOKEN:TOKEN + 1].bitcast(I32), 1 << 20).then_inc(blank_set, 1)
            for name, s in (("hid_ready", hid_ready), ("prob_ready", prob_ready), ("y_read", y_read),
                            ("y_ready", y_ready)):
                v.sem_inc(s, SEED[name])
            v.wait_ge(b1_turned, 1)
            v.tensor_copy(b1c[:], ps_T[:, 0, 0:E * KF]).then_inc(b1_ready, 1)
            v.wait_ge(first_loaded, 32)
            v.tensor_copy(whi[:, 0, :], raw[:]).then_inc(split, 1)
            v.wait_ge(split, 1)
            v.tensor_tensor(wlo[:, 0, :], raw[:], whi[:, 0, :].bitcast(F32), ALU.subtract).then_inc(split, 1)
            v.wait_ge(consts, 32)
            PER = 6

            def normalise(u):
                v.wait_ge(pay_loaded, 16 * (u + 1))
                v.tensor_copy(scales[:], pay[:, u % RING, :, MEAN:RSTD + 1]).then_inc(scales_ready, 1)
                v.wait_ge(scales_ready, u + 1)
                if not isinstance(u, int):
                    v.wait_ge(turned, u)
                for s in range(SUB):
                    last = v.tensor_scalar(hn[:, s, :], pay[:, u % RING, s, 0:D], scales[:, s, 0:1],
                                           scales[:, s, 1:2], ALU.subtract, ALU.mult)
                last.then_inc(hn_ready, 1)

            def lower(u):
                v.wait_ge(xhi_ready, u + 1)
                v.tensor_tensor(xlo[:], ps_T[:], xhi[:].bitcast(F32), ALU.subtract).then_inc(x_ready, 1)

            def expert(e, buf, begin, end):
                v.tensor_copy(b2e[:], b2b[:, bass.ds(e, 1), :].rearrange("p o d -> p (o d)")).then_inc(b2_own, 1)
                v.wait_ge(b2_own, e + 1)
                v.nop(nofuse=True)
                with v.Fori(begin, end) as u:
                    c = Count(u * PER)
                    normalise(u + 1)
                    for f in range(KF):
                        v.wait_ge(hhi_ready, KF * u + (f + 1))
                        v.tensor_tensor(hlo[:, f, :], hm[:, f, :], hhi[:, f, :].bitcast(F32), ALU.subtract)\
                            .then_inc(hid_ready, 1)
                    v.wait_ge(ex_ready, u + 1)
                    v.tensor_reduce(total[:], ex[:], AX.X, ALU.add).then_inc(step, c.inc())
                    lower(u + 1)
                    v.wait_ge(step, c.now())
                    v.reciprocal(prob[:], total[:]).then_inc(prob_ready, 1)
                    v.wait_ge(second_done, u + 1)
                    for s in range(SUB):
                        last = v.tensor_tensor(y[:, s, :], ps_Y[:, s, 0:D], b2e[:], ALU.add)
                    last.then_inc(y_read, 1)
                    v.wait_ge(prob_ready, u + 1 + SEED["prob_ready"])
                    v.wait_ge(y_read, u + 1 + SEED["y_read"])
                    for s in range(SUB):
                        last = v.tensor_scalar(y[:, s, :], y[:, s, :], prob[:, s:s + 1], None, ALU.mult)
                    last.then_inc(step, c.inc())
                    v.wait_ge(step, c.now())
                    v.tensor_scalar(finite[:], y[:], 0.0, 0.0, ALU.mult, ALU.is_equal)
                    v.tensor_scalar(low[:], y[:], 0.0, -HUGE, ALU.is_lt, ALU.mult).then_inc(step, c.inc())
                    v.wait_ge(y_clear, u + SEED["y_clear"])
                    v.tensor_copy(token[:], pay[:, u % RING, :, TOKEN].bitcast(I32))
                    v.tensor_scalar(yo[:], y[:], 0.0, HUGE, ALU.is_gt, ALU.mult).then_inc(step, c.inc())
                    v.wait_ge(step, c.now())
                    v.tensor_tensor(yo[:], yo[:], low[:], ALU.add).then_inc(step, c.inc())
                    v.wait_ge(step, c.now())
                    v.nop(nofuse=True)
                    v.copy_predicated(yo[:], finite[:], y[:]).then_inc(step, c.inc())
                    v.wait_ge(step, c.now())
                    v.tensor_tensor(yo[:], yo[:], pay[:, u % RING, :, 0:D], ALU.add).then_inc(y_ready, 1)
                    assert c.n == PER, c.n
            normalise(0)
            lower(0)
            experts(v, expert)

        @block.tensor
        def _(pe):
            pe.wait_ge(consts, 32)
            pe.transpose(ps_T[:, 0, 0:E * KF], b1r[:], ident[0:E * KF, 0:E * KF]).then_inc(b1_turned, 1)
            pe.wait_ge(b1_ready, 1)

            def transposes(u):
                pe.wait_ge(hn_ready, u + 1)
                if not isinstance(u, int):
                    pe.wait_ge(x_ready, u)
                for s in range(SUB):
                    for k in range(KD):
                        last = pe.transpose(ps_T[:, k, s * P:(s + 1) * P], hn[:, s, k * P:(k + 1) * P], ident[:])
                last.then_inc(turned, 1)

            transposes(0)

            def expert(e, buf, begin, end):
                pe.wait_ge(split, 2 * (e + 1))
                pe.nop(nofuse=True)
                with pe.Fori(begin, end) as u:
                    pe.wait_ge(x_ready, u + 1)
                    for f in range(KF):
                        pe.wait_ge(relu_done, KF * u + (f - 1 + SEED["relu_done"]))
                        passes = [(w, a, k) for k in range(KD) for w, a in ((whi, xhi), (whi, xlo), (wlo, xhi))]
                        for j, (w, a, k) in enumerate(passes):
                            last = pe.matmul(ps_H[:, f % 2, :], w1_at(w, buf, k, f), a[:, k, :],
                                             start=(j == 0), stop=(j == len(passes) - 1))
                        last.then_inc(first_done, 1)
                    transposes(u + 1)
                    pe.wait_ge(y_read, u + SEED["y_read"])
                    for f in range(KF):
                        pe.wait_ge(hid_ready, KF * u + (f + 1 + SEED["hid_ready"]))
                        for s in range(SUB):
                            cols = slice(s * P, (s + 1) * P)
                            for j, (a, w) in enumerate(((hhi, whi), (hhi, wlo), (hlo, whi))):
                                last = pe.matmul(ps_Y[:, s, 0:D], a[:, f, cols], w2_at(w, buf, f),
                                                 start=(f == 0 and j == 0), stop=(f == KF - 1 and j == 2))
                    last.then_inc(second_done, 1)
            experts(pe, expert)


def build_program(nc, x, src, dst, edge_weight, gate_w, gate_b, w1, b1, w2, b2, out):
    N, D = x.shape
    E = gate_w.shape[1]
    C = max(1, math.ceil(CAPACITY_FACTOR * N / E))
    UNIT = 4 * P
    UMAX = -(-C // UNIT)
    QUEUE = (UMAX + 1) * UNIT
    W = LOGIT + E
    AGG = -(-(N + STEP) // (16 * P)) * (16 * P)
    t = dict(x=x, src=src, dst=dst, weight=edge_weight, gate_w=gate_w, gate_b=gate_b, w1=w1, b1=b1,
             w2=w2, b2=b2, out=out, C=C, QUEUE=QUEUE, UNIT=UNIT, UMAX=UMAX)
    t["agg"] = nc.dram_tensor("agg", (AGG, D), F16, kind="Internal").ap()
    t["slots"] = nc.dram_tensor("slots", (E * QUEUE, W), F32, kind="Internal").ap()
    with ExitStack() as outer:
        t["ident"] = outer.enter_context(nc.sbuf_tensor("ident", [P, P], F32))
        t["before"] = outer.enter_context(nc.sbuf_tensor("before", [P, P], F16))
        t["ones"] = outer.enter_context(nc.sbuf_tensor("ones", [P, P], F16))
        t["eps"] = outer.enter_context(nc.sbuf_tensor("eps", [P, 1], F32))
        for name, n in (("first_unit", E + 1), ("first_row", E), ("first_blank", E)):
            t[name] = outer.enter_context(nc.sbuf_tensor(name, [1, n], I32))
        for phase in (edge_and_constants, route_tokens, run_experts):
            with ExitStack() as ctx:
                phase(nc, ctx, t)


_INS = ["x", "src", "dst", "edge_weight", "L0_ffn_gate_w", "L0_ffn_gate_b", "L0_ffn_w1", "L0_ffn_b1",
        "L0_ffn_w2", "L0_ffn_b2"]


def kernel(**inputs):
    import numpy as _np
    import concourse.bacc as _bacc
    from concourse import mybir as _mybir
    from concourse.bass_utils import run_bass_kernel_spmd as _run

    nc = _bacc.Bacc("TRN2", target_bir_lowering=False, num_devices=1)
    arrays, args = {}, []
    for name in _INS:
        a = _np.ascontiguousarray(inputs[name])
        arrays[f"in_{name}"] = a
        args.append(nc.dram_tensor(f"in_{name}", a.shape, _mybir.dt.from_np(a.dtype), kind="ExternalInput").ap())
    out = nc.dram_tensor("out_x", inputs["x"].shape, _mybir.dt.float32, kind="ExternalOutput").ap()
    build_program(nc, *args, out)
    r = _run(nc, [arrays], core_ids=[0])
    return r.results[0]["out_x"]
```

```python
import math
from contextlib import ExitStack

import concourse.bass as bass
from concourse import mybir

ALU = mybir.AluOpType
ACT = mybir.ActivationFunctionType
AX = mybir.AxisListType
F32 = mybir.dt.float32
F32R = mybir.dt.float32r
F16 = mybir.dt.float16
I32 = mybir.dt.int32
U8 = mybir.dt.uint8

P = 128
G = 8
STEP = G * P
EPS = 1e-5
CAPACITY_FACTOR = 1.25
FLAG = float(1 << 20)

MEAN, RSTD, TOKEN, LOGIT = 256, 257, 258, 259
RING = 4


class Count:

    def __init__(self, base):
        self.base, self.n = base, 0

    def inc(self):
        self.n += 1
        return 1

    def now(self):
        return self.base + self.n


HOLD = 6
INPUTS = 3


def steps(eng, total, unroll, body):
    for r in range(unroll):
        body(0, r)
    with eng.Fori(1, total // unroll) as i:
        for r in range(unroll):
            body(i, r)
    for r in range(total % unroll):
        body(total // unroll, r)


def edge_and_constants(nc, ctx, t):
    x, src, dst, weight = t["x"], t["src"], t["dst"], t["weight"]
    agg = t["agg"]
    N, D = x.shape
    M = src.shape[0]
    S = -(-M // STEP)
    LAST = S - 1
    REPEATED = S * STEP - M
    assert REPEATED < STEP and LAST % HOLD == 0

    def base_of(i, r):
        return M - STEP if (isinstance(i, int) and HOLD * i + r == LAST) else i * (HOLD * STEP) + r * STEP

    def sb(name, shape, dt):
        return ctx.enter_context(nc.sbuf_tensor(name, shape, dt))

    def sem(name):
        return ctx.enter_context(nc.semaphore(name))

    zeros = sb("zeros16", [P, 16 * D], F16)
    src_row = sb("src_row", [P, INPUTS, STEP], I32)
    src_col = sb("src_col", [P, INPUTS, G], I32)
    dst_col = sb("dst_col", [P, INPUTS, G], I32)
    w_col = sb("w_col", [P, INPUTS, G], F32)
    w16 = sb("w16", [P, 2, G], F16)
    w32 = sb("w32", [P, 2, G], F32)
    srcf = sb("srcf", [P, 2, G], F32)
    rows = sb("rows", [P, INPUTS, G, D], F32)
    same = sb("same", [P, 2, G, STEP], F16)
    earlier = sb("earlier", [P, 2, G, P], F16)
    stats = sb("e_stats", [P, G, 6], F32)
    mv = sb("e_mv", [P, 2, G, 2], F32)
    std = sb("e_std", [P, 2, G], F32)
    rstd = sb("e_rstd", [P, 2, G], F32)
    offset = sb("e_offset", [P, 2, G], F32)
    msg = sb("msg", [P, 2, G, D], F16)
    norm16 = sb("norm16", [P, 2, G, D], F16)
    sums = sb("sums", [P, HOLD, G, D], F16)
    spare_i = sb("spare_i", [P, G], I32)
    spare = sb("spare", [P, G], F32)
    shift = sb("shift", [P, G], F32)
    target = sb("target", [P, HOLD, G], I32)
    ones, before, ident, eps = t["ones"], t["before"], t["ident"], t["eps"]

    ps_sum = ctx.enter_context(nc.psum_tensor("ps_sum", [P, G, D], F32))
    ps_cnt = ctx.enter_context(nc.psum_tensor("ps_cnt", [P, 512], F32))

    weights_loaded = sem("weights_loaded")
    set_up = sem("set_up")
    pool_set = sem("pool_set")
    agg_zeroed = sem("agg_zeroed")
    idx_loaded = [sem(f"idx_loaded{r}") for r in range(INPUTS)]
    gathered = [sem(f"gathered{r}") for r in range(INPUTS)]
    added = [sem(f"added{r}") for r in range(HOLD)]
    masks_ready = sem("masks_ready")
    stats_ready = sem("e_stats_ready")
    std_ready = sem("e_std_ready")
    scale_ready = sem("scale_ready")
    norm_done = sem("norm_done")
    msg_ready = sem("msg_ready")
    counted = sem("counted")
    summed = sem("summed")
    sums_out = sem("sums_out")
    edge_done = sem("edge_done")
    step = sem("e_step")

    BANKS = G * D // 512
    PER_BANK = G // BANKS
    AHEAD = HOLD - 1
    turn = lambda i, r: (HOLD // INPUTS) * i + r // INPUTS
    row_view = lambda ap: ap.rearrange("(p c) -> p c", c=G)
    agg_v = agg.rearrange("(p b r) d -> b p (r d)", p=P, r=16)
    ZEROS = agg_v.shape[0]
    assert S // HOLD >= 2

    with nc.Block() as block:

        @block.sync
        def _(sp):
            def load(i, r):
                s, h = HOLD * i + r, r % INPUTS
                if not (isinstance(i, int) and s < INPUTS):
                    sp.wait_ge(edge_done, s + 1 - INPUTS)
                b = base_of(i, r)
                sp.dma_start(dst_col[:, h, :], row_view(dst[bass.ds(b, STEP)])).then_inc(idx_loaded[h], 16)
                sp.dma_start(src_col[:, h, :], row_view(src[bass.ds(b, STEP)])).then_inc(idx_loaded[h], 16)
                sp.dma_start(w_col[:, h, :], row_view(weight[bass.ds(b, STEP)])).then_inc(idx_loaded[h], 16)
                sp.dma_start(src_row[:, h, :], src[bass.ds(b, STEP)].partition_broadcast(P))\
                    .then_inc(idx_loaded[h], 16)
            steps(sp, S, HOLD, load)
            w1, w2, raw = t["w1"], t["w2"], t["raw"]
            WF = raw.shape[1] // 2
            sp.dma_start(raw[:, 0:WF].rearrange("p (k f) -> p k f", k=w1.shape[1] // P),
                         w1[0].rearrange("(k p) f -> p k f", p=P)).then_inc(weights_loaded, 16)
            sp.dma_start(raw[:, WF:2 * WF].rearrange("p (k d) -> p k d", k=w2.shape[1] // P),
                         w2[0].rearrange("(k p) d -> p k d", p=P)).then_inc(weights_loaded, 16)
            sp.wait_ge(weights_loaded, 32)

        @block.gpsimd
        def _(pool):
            pool.memset(before[:], 1.0).then_inc(pool_set, 1)
            pool.memset(ident[:], 0.0).then_inc(pool_set, 1)
            pool.iota(spare_i[:], [[P, G]], base=N, channel_multiplier=1).then_inc(pool_set, 1)
            pool.wait_ge(pool_set, 3)
            pool.affine_select(out=before[:], in_=before[:], compare_op=ALU.is_gt, fill=0.0, base=0,
                               pattern=[[1, P]], channel_multiplier=-1).then_inc(pool_set, 1)
            pool.affine_select(out=ident[:], in_=ident[:], compare_op=ALU.not_equal, fill=1.0, base=0,
                               pattern=[[-1, P]], channel_multiplier=1).then_inc(pool_set, 1)

            def gather(i, r):
                s, h = HOLD * i + r, r % INPUTS
                pool.wait_ge(idx_loaded[h], 64 * (turn(i, r) + 1))
                pool.nop(nofuse=True)
                if not (isinstance(i, int) and s < INPUTS):
                    pool.wait_ge(edge_done, s + 1 - INPUTS)
                    pool.nop(nofuse=True)
                for c in range(G):
                    pool.indirect_dma_start(
                        out=rows[:, h, c, :], out_offset=None, in_=x[:, :],
                        in_offset=bass.IndirectOffsetOnAxis(ap=dst_col[:, h, c:c + 1], axis=0),
                    ).then_inc(gathered[h], 16)

            def scatter(i, r):
                s = HOLD * i + r
                pool.wait_ge(edge_done, s + 1)
                pool.wait_ge(sums_out, BANKS * (s + 1))
                pool.nop(nofuse=True)
                if isinstance(i, int) and s == 0:
                    pool.wait_ge(agg_zeroed, 16 * ZEROS)
                else:
                    pool.wait_ge(added[r - 1], 16 * G * (i + 1 if r else i))
                    pool.nop(nofuse=True)
                for c in range(G):
                    pool.indirect_dma_start(
                        out=agg[:, :], out_offset=bass.IndirectOffsetOnAxis(ap=target[:, r, c:c + 1], axis=0),
                        in_=sums[:, r, c, :], in_offset=None, compute_op=ALU.add,
                    ).then_inc(added[r], 16)

            for r in range(AHEAD):
                gather(0, r)
            gather(0, AHEAD)
            scatter(0, 0)
            for r in range(1, HOLD):
                gather(1, r - 1)
                scatter(0, r)
            with pool.Fori(1, S // HOLD - 1) as i:
                gather(i, AHEAD)
                scatter(i, 0)
                for r in range(1, HOLD):
                    gather(i + 1, r - 1)
                    scatter(i, r)
            n = S // HOLD - 1
            gather(n, AHEAD)
            scatter(n, 0)
            gather(n + 1, 0)
            for r in range(1, HOLD):
                scatter(n, r)
            scatter(n + 1, 0)
            for r in range(HOLD):
                pool.wait_ge(added[r], 16 * G * (n + (2 if r == 0 else 1)))

        @block.scalar
        def _(act):
            act.wait_ge(set_up, 2)
            parts = iter(range(ZEROS))

            def zero(i, count=1):
                for _ in range(count if isinstance(i, int) and i == 0 else 0):
                    b = next(parts, None)
                    if b is not None:
                        act.dma_start(agg_v[b], zeros[:]).then_inc(agg_zeroed, 16)

            zero(0, 2 + max(0, ZEROS - AHEAD * (BANKS + 2)))

            def body(i, r):
                s, h, q = HOLD * i + r, r % 2, r % INPUTS
                zero(i)
                act.wait_ge(stats_ready, s + 1)
                act.activation(std[:, h, :], mv[:, h, :, 1], ACT.Sqrt, bias=eps[:, 0:1]).then_inc(std_ready, 1)
                zero(i)
                act.wait_ge(scale_ready, s + 1)
                if not (isinstance(i, int) and s < 2):
                    act.wait_ge(msg_ready, s - 1)
                for c in range(G):
                    last = act.activation(norm16[:, h, c, :], rows[:, q, c, :], ACT.Identity,
                                          bias=offset[:, h, c:c + 1], scale=rstd[:, h, c:c + 1])
                last.then_inc(norm_done, 1)
                if not (isinstance(i, int) and i == 0):
                    act.wait_ge(added[r], 16 * G * i)
                for b in range(BANKS):
                    zero(i)
                    act.wait_ge(summed, BANKS * s + b + 1)
                    part = slice(b * PER_BANK, (b + 1) * PER_BANK)
                    act.activation(sums[:, r, part, :], ps_sum[:, part, :], ACT.Copy).then_inc(sums_out, 1)
            steps(act, S, HOLD, body)
            assert next(parts, None) is None

        @block.vector
        def _(v):
            v.memset(zeros[:], 0.0).then_inc(set_up, 1)
            v.memset(eps[:], EPS).then_inc(set_up, 1)
            v.memset(ones[:], 1.0)
            v.wait_ge(pool_set, 5)
            v.tensor_copy(spare[:], spare_i[:]).then_inc(step, 1)
            v.wait_ge(step, 1)
            SET, PER = 1, 6

            def masks(h, q, chunks):
                for c in chunks:
                    last = v.tensor_scalar(same[:, h, c, :], src_row[:, q, :], srcf[:, h, c:c + 1], None,
                                           ALU.is_equal)
                return last

            def body(i, r):
                s, h, q = HOLD * i + r, r % 2, r % INPUTS
                n = Count(s * PER + SET)
                v.wait_ge(idx_loaded[q], 64 * (turn(i, r) + 1))
                v.tensor_copy(srcf[:, h, :], src_col[:, q, :])
                v.tensor_copy(w16[:, h, :], w_col[:, q, :]).then_inc(step, n.inc())
                v.wait_ge(gathered[q], 16 * G * (turn(i, r) + 1))
                for c in range(G):
                    last = v.bn_stats(stats[:, c, :], rows[:, q, c, :])
                last.then_inc(step, n.inc())
                v.wait_ge(step, n.now())
                v.nop(nofuse=True)
                for c in range(G):
                    last = v.bn_aggr(mv[:, h, c, :], stats[:, c, :])
                last.then_inc(stats_ready, 1)
                v.tensor_copy(w32[:, h, :], w16[:, h, :])
                v.tensor_tensor(shift[:], spare[:], srcf[:, h, :], ALU.subtract).then_inc(step, n.inc())
                if isinstance(i, int) and s == LAST and REPEATED:
                    assert REPEATED % G == 0
                    v.wait_ge(step, n.now())
                    v.memset(w32[0:REPEATED // G, h, :], 0.0).then_inc(step, 1)
                    n.base += 1
                if not (isinstance(i, int) and s < 2):
                    v.wait_ge(summed, BANKS * (s - 1))
                masks(h, q, range(G // 2))
                v.wait_ge(std_ready, s + 1)
                v.reciprocal(rstd[:, h, :], std[:, h, :]).then_inc(step, n.inc())
                masks(h, q, range(G // 2, G // 2 + 1))
                v.wait_ge(step, n.now())
                v.scalar_tensor_tensor(out=offset[:, h, :], in0=mv[:, h, :, 0], scalar=-1.0, in1=rstd[:, h, :],
                                       op0=ALU.mult, op1=ALU.mult).then_inc(scale_ready, 1)
                masks(h, q, range(G // 2 + 1, G)).then_inc(step, n.inc())
                v.wait_ge(step, n.now())
                for c in range(G):
                    last = v.tensor_tensor(earlier[:, h, c, :],
                                           same[:, h, c, :].rearrange("j (p a) -> j a p", a=G)[:, c, :],
                                           before[:], ALU.mult)
                last.then_inc(masks_ready, 1)
                v.wait_ge(norm_done, s + 1)
                for c in range(G):
                    last = v.tensor_scalar(msg[:, h, c, :], norm16[:, h, c, :], w32[:, h, c:c + 1], None, ALU.mult)
                last.then_inc(msg_ready, 1)
                v.wait_ge(counted, s + 1)
                v.scalar_tensor_tensor(out=shift[:], in0=ps_cnt[:, 0:G], scalar=0.5, in1=shift[:],
                                       op0=ALU.is_gt, op1=ALU.mult).then_inc(step, n.inc())
                v.wait_ge(step, n.now())
                if not (isinstance(i, int) and i == 0):
                    v.wait_ge(added[r], 16 * G * i)
                v.tensor_tensor(target[:, r, :], shift[:], srcf[:, h, :], ALU.add).then_inc(edge_done, 1)
                assert n.n == PER, n.n
            steps(v, S, HOLD, body)

        @block.tensor
        def _(pe):
            def body(i, r):
                s, h = HOLD * i + r, r % 2
                seen = lambda b, c: same[:, h, b, :].rearrange("j (p a) -> j a p", a=G)[:, c, :]
                pe.wait_ge(masks_ready, s + 1)
                if not (isinstance(i, int) and s == 0):
                    pe.wait_ge(edge_done, s)
                for c in range(G):
                    for b in range(c):
                        pe.matmul(ps_cnt[:, c:c + 1], seen(b, c), ones[:, 0:1], start=(b == 0), stop=False)
                    last = pe.matmul(ps_cnt[:, c:c + 1], earlier[:, h, c, :], ones[:, 0:1],
                                     start=(c == 0), stop=True)
                last.then_inc(counted, 1)
                pe.wait_ge(msg_ready, s + 1)
                for k in range(BANKS):
                    if not (isinstance(i, int) and s == 0):
                        pe.wait_ge(sums_out, BANKS * (s - 1) + k + 1)
                    for c in range(k * PER_BANK, (k + 1) * PER_BANK):
                        for b in range(G):
                            last = pe.matmul(ps_sum[:, c, :], seen(b, c), msg[:, h, b, :],
                                             start=(b == 0), stop=(b == G - 1))
                    last.then_inc(summed, 1)
            steps(pe, S, HOLD, body)


def route_tokens(nc, ctx, t):
    x, agg, slots, out = t["x"], t["agg"], t["slots"], t["out"]
    gate_w, gate_b = t["gate_w"], t["gate_b"]
    N, D = x.shape
    E = gate_w.shape[1]
    KD = D // P
    W = slots.shape[1]
    C, QUEUE = t["C"], t["QUEUE"]
    S = -(-N // STEP)
    LAST = S - 1
    REPEATED = S * STEP - N
    assert LAST % RING == 0

    def base_of(i, r):
        s = RING * i + r
        return N - STEP if (isinstance(i, int) and s == LAST) else i * (RING * STEP) + r * STEP

    def sb(name, shape, dt):
        return ctx.enter_context(nc.sbuf_tensor(name, shape, dt))

    def sem(name):
        return ctx.enter_context(nc.semaphore(name))

    xt = sb("xt", [P, 2, G, D], F32)
    at = sb("at", [P, 2, G, D], F16)
    pay = sb("pay", [P, RING, G, W], F32)
    h = sb("h", [P, 2, G, D], F32)
    hT = sb("hT", [P, G * KD, P], F32)
    gw = sb("gw", [P, KD, E], F32)
    gb = sb("gb", [P, E], F32)
    stats = sb("t_stats", [P, G, 6], F32)
    mv = sb("t_mv", [P, 2, G, 2], F32)
    std = sb("t_std", [P, 2, G], F32)
    shift = sb("t_shift", [P, 2, G], F32)
    token_i = sb("token_i", [P, G], I32)
    token = sb("token", [P, G], F32)
    expert_i = sb("expert_i", [P, E], I32)
    expert = sb("expert", [P, E], F32)
    prefer = sb("prefer", [P, E], F32)
    limit = sb("limit", [P, E], F32)
    fresh = sb("fresh", [P, G], F16)
    lg = sb("lg", [P, G, E], F32)
    cand = sb("cand", [P, G, E], F32)
    top = sb("top", [P, G], F32)
    best = sb("best", [P, G], F32)
    hot = sb("hot", [P, 2, G, E], F16)
    place = sb("place", [P, 2, G + 1, E], F32)
    kept_hot = sb("kept_hot", [P, G, E], F32)
    own = sb("own", [P, G, E], F32)
    kept = sb("kept", [P, G], F32)
    where = sb("where", [P, G], F32)
    slot_i = sb("slot_i", [P, RING, G], I32)
    ones, before, ident, eps = t["ones"], t["before"], t["ident"], t["eps"]

    ps_T = ctx.enter_context(nc.psum_tensor("ps_T", [P, G * KD, P], F32))
    ps_L = ctx.enter_context(nc.psum_tensor("ps_L", [P, 512], F32))
    ps_R = ctx.enter_context(nc.psum_tensor("ps_R", [P, 512], F32))
    logits = ps_L[:, 0:G * E].rearrange("p (g e) -> p g e", g=G)
    ranks = ps_R[:, 0:(G + 1) * E].rearrange("p (g e) -> p g e", g=G + 1)

    bound_i = sb("bound_i", [1, E, t["UMAX"]], I32)
    filled = sb("filled", [1, E], F32)
    queued = sb("queued", [1, E], F32)
    over = sb("over", [1, E, t["UMAX"]], F32)
    count = sb("count", [1, E], F32)
    begin = sb("begin", [1, E + 1], F32)
    offset = sb("offset", [1, E], F32)
    first_unit, first_row, first_blank = t["first_unit"], t["first_row"], t["first_blank"]

    consts = sem("t_consts")
    split = sem("t_split")
    pool_set = sem("t_pool_set")
    loaded = [sem(f"t_loaded{r}") for r in range(2)]
    x1_ready = sem("x1_ready")
    stats_ready = sem("t_stats_ready")
    std_ready = sem("t_std_ready")
    norm_ready = sem("norm_ready")
    h_ready = sem("h_ready")
    turned = sem("turned")
    hT_ready = sem("hT_ready")
    gated = sem("gated")
    hot_ready = sem("hot_ready")
    ranked = sem("ranked")
    slot_ready = sem("slot_ready")
    out_written = [sem(f"out_written{r}") for r in range(RING)]
    sent = [sem(f"sent{r}") for r in range(RING)]
    step = sem("t_step")
    step_b = sem("t_step_b")

    BANKS = G * KD * P // 512
    PER_BANK = G * KD // BANKS

    with nc.Block() as block:

        @block.sync
        def _(sp):
            sp.dma_start(gw[:], gate_w.rearrange("(k p) e -> p k e", p=P)).then_inc(consts, 16)
            sp.dma_start(gb[:], gate_b.partition_broadcast(P)).then_inc(consts, 16)

            def load(i, r):
                s = RING * i + r
                if not (isinstance(i, int) and s < 2):
                    sp.wait_ge(x1_ready, s - 1)
                b = base_of(i, r)
                sp.dma_start(xt[:, r % 2], x[bass.ds(b, STEP), :].rearrange("(g p) d -> p g d", p=P))\
                    .then_inc(loaded[r % 2], 16)
                sp.dma_start(at[:, r % 2], agg[bass.ds(b, STEP), :].rearrange("(g p) d -> p g d", p=P))\
                    .then_inc(loaded[r % 2], 16)

            def store(i, r, b):
                sp.wait_ge(x1_ready, RING * i + r + 1)
                sp.dma_start(out[bass.ds(b, STEP), :].rearrange("(g p) d -> p g d", p=P), pay[:, r, :, 0:D])\
                    .then_inc(out_written[r], 16)

            load(0, 0)
            for r in range(1, RING):
                load(0, r)
                store(0, r - 1, base_of(0, r - 1))
            with sp.Fori(1, S // RING) as i:
                for r in range(RING):
                    load(i, r)
                    if r:
                        store(i, r - 1, base_of(i, r - 1))
                    else:
                        store(i - 1, RING - 1, base_of(i - 1, RING - 1))
            n = S // RING
            load(n, 0)
            store(n - 1, RING - 1, base_of(n - 1, RING - 1))
            sp.wait_ge(out_written[RING - 1], 16 * n)
            store(n, 0, base_of(n, 0))
            for r in range(RING):
                sp.wait_ge(out_written[r], 16 * (n + (r == 0)))

        @block.gpsimd
        def _(pool):
            pool.iota(token_i[:], [[P, G]], base=0, channel_multiplier=1).then_inc(pool_set, 1)
            pool.iota(expert_i[:], [[1, E]], base=0, channel_multiplier=0).then_inc(pool_set, 1)
            pool.iota(bound_i[:], [[0, E], [t["UNIT"], t["UMAX"]]], base=0, channel_multiplier=0)\
                .then_inc(pool_set, 1)
            pool.memset(fresh[:], 1.0).then_inc(pool_set, 1)
            pool.wait_ge(pool_set, 4)
            pool.affine_select(out=fresh[:], in_=fresh[:], compare_op=ALU.is_ge, fill=0.0, base=-REPEATED,
                               pattern=[[P, G]], channel_multiplier=1).then_inc(pool_set, 1)

            def body(i, r):
                pool.wait_ge(slot_ready, RING * i + r + 1)
                pool.nop(nofuse=True)
                for g in range(G):
                    pool.indirect_dma_start(
                        out=slots[:, :], out_offset=bass.IndirectOffsetOnAxis(ap=slot_i[:, r, g:g + 1], axis=0),
                        in_=pay[:, r, g, :], in_offset=None, bounds_check=E * QUEUE - 1, oob_is_err=False,
                    ).then_inc(sent[r], 16)
            steps(pool, S, RING, body)
            for r in range(RING):
                pool.wait_ge(sent[r], 16 * G * (S // RING + (r < S % RING)))

        @block.scalar
        def _(act):
            def body(i, r):
                s = RING * i + r
                q = r % 2
                act.wait_ge(stats_ready, s + 1)
                act.activation(std[:, q, :], mv[:, q, :, 1], ACT.Sqrt, bias=eps[:, 0:1]).then_inc(std_ready, 1)
                act.wait_ge(norm_ready, s + 1)
                if not (isinstance(i, int) and s < 2):
                    act.wait_ge(turned, BANKS * (s - 1))
                act.nop(nofuse=True)

                def copy(k):
                    if k == 0 and not (isinstance(i, int) and s < 1):
                        act.wait_ge(gated, s)
                    act.wait_ge(turned, BANKS * s + k + 1)
                    part = slice(k * PER_BANK, (k + 1) * PER_BANK)
                    act.activation(hT[:, part, :], ps_T[:, part, :], ACT.Copy).then_inc(hT_ready, 1)

                for k in range(BANKS):
                    for g in range(k * G // BANKS, (k + 1) * G // BANKS):
                        last = act.activation(h[:, q, g, :], pay[:, r, g, 0:D], ACT.Identity,
                                              bias=shift[:, q, g:g + 1], scale=pay[:, r, g, RSTD:RSTD + 1])
                    last.then_inc(h_ready, 1)
                    if k:
                        copy(k - 1)
                copy(BANKS - 1)
            steps(act, S, RING, body)

        @block.tensor
        def _(pe):
            def rank(i, r):
                s = RING * i + r
                q = r % 2
                pe.wait_ge(hot_ready, s + 1)
                if not (isinstance(i, int) and s < 1):
                    pe.wait_ge(slot_ready, s)
                pe.matmul(ranks[:, 0:G, :], before[:], hot[:, q], start=True, stop=False, skip_group_check=True)
                for g in range(G):
                    last = pe.matmul(ranks[:, g + 1:G + 1, :], ones[:],
                                     hot[:, q, g, :].unsqueeze(1).broadcast_to([P, G - g, E]),
                                     start=False, stop=(g == G - 1), skip_group_check=True)
                last.then_inc(ranked, 1)

            def gate(s, k, i):
                pe.wait_ge(hT_ready, BANKS * s + k + 1)
                if not (isinstance(i, int) and isinstance(s, int) and s < 1):
                    pe.wait_ge(hot_ready, s)
                else:
                    pe.wait_ge(consts, 32)
                for g in range(k * G // BANKS, (k + 1) * G // BANKS):
                    for kd in range(KD):
                        last = pe.matmul(logits[:, g, :], hT[:, g * KD + kd, :], gw[:, kd, :],
                                         start=(kd == 0), stop=(kd == KD - 1))
                if k == BANKS - 1:
                    last.then_inc(gated, 1)

            def body(i, r):
                s = RING * i + r
                q = r % 2
                for k in range(BANKS):
                    pe.wait_ge(h_ready, BANKS * s + k + 1)
                    if not (isinstance(i, int) and s < 1):
                        pe.wait_ge(hT_ready, BANKS * (s - 1) + k + 1)
                    for n in range(k * PER_BANK, (k + 1) * PER_BANK):
                        g, kd = divmod(n, KD)
                        last = pe.transpose(ps_T[:, n, :], h[:, q, g, kd * P:(kd + 1) * P], ident[:])
                    last.then_inc(turned, 1)
                    if k == 1 and not (isinstance(i, int) and s < 1):
                        rank(*((i, r - 1) if r else (i - 1, RING - 1)))
                    if k:
                        gate(s, k - 1, i)
                gate(s, BANKS - 1, i)
            steps(pe, S, RING, body)
            rank(LAST // RING, 0)

        @block.vector
        def _(v):
            v.wait_ge(pool_set, 5)
            raw, whi, wlo = t["raw"], t["whi"], t["wlo"]
            v.tensor_copy(whi[:, 0, :], raw[:]).then_inc(split, 1)
            v.wait_ge(split, 1)
            v.tensor_tensor(wlo[:, 0, :], raw[:], whi[:, 0, :].bitcast(F32), ALU.subtract)
            v.tensor_copy(token[:], token_i[:])
            v.tensor_copy(expert[:], expert_i[:]).then_inc(step, 1)
            v.wait_ge(step, 1)
            v.tensor_scalar(prefer[:], expert[:], -1.0, float(E), ALU.mult, ALU.add)
            v.tensor_scalar(limit[:], expert[:], float(QUEUE), float(C), ALU.mult, ALU.add)
            v.tensor_scalar(place[:, 1, G, :], expert[:], float(QUEUE), None, ALU.mult).then_inc(step, 1)
            v.wait_ge(step, 2)
            v.wait_ge(consts, 32)
            SET, PER_A, PER_B, CHOICE = 2, 4, 12, 6

            def steps_before(i, r, back):
                return (i, r - back) if r >= back else (i - 1, r - back + RING)

            def statistics(i, r, n):
                s = RING * i + r
                q = r % 2
                last_step = isinstance(i, int) and s == LAST
                v.wait_ge(loaded[q], 32 * ((RING // 2) * i + r // 2 + 1))
                if not (isinstance(i, int) and i == 0):
                    v.wait_ge(sent[r], 16 * G * i)
                    v.wait_ge(out_written[r], 16 * i)
                v.tensor_tensor(pay[:, r, :, 0:D], xt[:, q], at[:, q], ALU.add).then_inc(x1_ready, 1)
                if not (isinstance(i, int) and s < 2):
                    slot(*steps_before(i, r, 2), Count((s - 2) * PER_B + CHOICE))
                v.wait_ge(x1_ready, s + 1)
                for g in range(G):
                    last = v.bn_stats(stats[:, g, :], pay[:, r, g, 0:D])
                last.then_inc(step, n.inc())
                if last_step:
                    v.tensor_scalar(token[:], token[:], -float(REPEATED), None, ALU.add).then_inc(step, n.inc())
                else:
                    v.engine_nop().then_inc(step, n.inc())
                v.wait_ge(step, n.now())
                v.nop(nofuse=True)
                for g in range(G):
                    last = v.bn_aggr(mv[:, q, g, :], stats[:, g, :])
                last.then_inc(stats_ready, 1)

            def scales(i, r, n):
                s = RING * i + r
                q = r % 2
                v.tensor_copy(pay[:, r, :, TOKEN].bitcast(I32), token[:]).then_inc(step, n.inc())
                v.wait_ge(step, n.now())
                v.tensor_scalar(token[:], token[:], float(STEP), None, ALU.add)
                v.tensor_copy(pay[:, r, :, MEAN], mv[:, q, :, 0])
                v.wait_ge(std_ready, s + 1)
                v.reciprocal(pay[:, r, :, RSTD], std[:, q, :]).then_inc(step, n.inc())
                v.wait_ge(step, n.now())
                v.scalar_tensor_tensor(out=shift[:, q, :], in0=mv[:, q, :, 0], scalar=-1.0,
                                       in1=pay[:, r, :, RSTD], op0=ALU.mult, op1=ALU.mult)\
                    .then_inc(norm_ready, 1)
                assert n.n == PER_A, n.n

            def choice(i, r, n):
                s = RING * i + r
                q = r % 2
                last_step = isinstance(i, int) and s == LAST
                v.wait_ge(gated, s + 1)
                v.tensor_tensor(lg[:], logits, gb[:].unsqueeze(1).broadcast_to([P, G, E]), ALU.add)\
                    .then_inc(step_b, n.inc())
                v.wait_ge(step_b, n.now())
                v.tensor_reduce(top[:], lg[:], AX.X, ALU.max).then_inc(step_b, n.inc())
                v.wait_ge(step_b, n.now())
                less = pay[:, r, :, LOGIT:LOGIT + E]
                v.tensor_tensor(less, lg[:], top[:].unsqueeze(2).broadcast_to([P, G, E]), ALU.subtract)\
                    .then_inc(step_b, n.inc())
                v.wait_ge(step_b, n.now())
                v.scalar_tensor_tensor(out=cand[:], in0=less, scalar=0.0,
                                       in1=prefer[:].unsqueeze(1).broadcast_to([P, G, E]),
                                       op0=ALU.is_equal, op1=ALU.mult).then_inc(step_b, n.inc())
                v.wait_ge(step_b, n.now())
                v.tensor_reduce(best[:], cand[:], AX.X, ALU.max).then_inc(step_b, n.inc())
                v.wait_ge(step_b, n.now())
                if last_step:
                    v.tensor_tensor(own[:], cand[:], best[:].unsqueeze(2).broadcast_to([P, G, E]), ALU.is_equal)\
                        .then_inc(step_b, n.inc())
                    v.wait_ge(step_b, n.now())
                    v.tensor_tensor(hot[:, q], own[:], fresh[:].unsqueeze(2).broadcast_to([P, G, E]), ALU.mult)\
                        .then_inc(hot_ready, 1)
                else:
                    v.tensor_tensor(hot[:, q], cand[:], best[:].unsqueeze(2).broadcast_to([P, G, E]), ALU.is_equal)\
                        .then_inc(hot_ready, 1)
                    v.engine_nop().then_inc(step_b, n.inc())

            def slot(i, r, n):
                s = RING * i + r
                q = r % 2
                v.wait_ge(ranked, s + 1)
                v.wait_ge(hot_ready, s + 1)
                v.tensor_tensor(place[:, q], ranks, place[:, 1 - q, G, :].unsqueeze(1).broadcast_to([P, G + 1, E]),
                                ALU.add).then_inc(step_b, n.inc())
                v.wait_ge(step_b, n.now())
                v.tensor_tensor(kept_hot[:], place[:, q, 0:G, :], limit[:].unsqueeze(1).broadcast_to([P, G, E]),
                                ALU.is_lt)
                v.tensor_tensor(own[:], place[:, q, 0:G, :], hot[:, q], ALU.mult).then_inc(step_b, n.inc())
                v.wait_ge(step_b, n.now())
                v.tensor_tensor(kept_hot[:], kept_hot[:], hot[:, q], ALU.mult).then_inc(step_b, n.inc())
                v.tensor_reduce(where[:], own[:], AX.X, ALU.add).then_inc(step_b, n.inc())
                v.wait_ge(step_b, n.now())
                v.tensor_reduce(kept[:], kept_hot[:], AX.X, ALU.add).then_inc(step_b, n.inc())
                v.wait_ge(step_b, n.now())
                v.scalar_tensor_tensor(out=where[:], in0=kept[:], scalar=-FLAG, in1=where[:],
                                       op0=ALU.mult, op1=ALU.add).then_inc(step_b, n.inc())
                v.wait_ge(step_b, n.now())
                v.tensor_scalar(slot_i[:, r, :], where[:], FLAG, None, ALU.add).then_inc(slot_ready, 1)
                assert n.n == PER_B - CHOICE, n.n

            def body(i, r):
                s = RING * i + r
                a = Count(s * PER_A + SET)
                statistics(i, r, a)
                scales(i, r, a)
                if not (isinstance(i, int) and s == 0):
                    choice(*steps_before(i, r, 1), Count((s - 1) * PER_B))
            steps(v, S, RING, body)
            n = LAST // RING
            slot(*steps_before(n, 0, 1), Count((LAST - 1) * PER_B + CHOICE))
            choice(n, 0, Count(LAST * PER_B))
            slot(n, 0, Count(LAST * PER_B + CHOICE))
            n = Count(S * PER_A + SET)
            v.wait_ge(slot_ready, S)
            v.tensor_tensor(filled[:], place[0:1, LAST % 2, G, :], limit[0:1, :], ALU.min).then_inc(step, n.inc())
            v.wait_ge(step, n.now())
            v.scalar_tensor_tensor(out=queued[:], in0=expert[0:1, :], scalar=-float(QUEUE), in1=filled[:],
                                   op0=ALU.mult, op1=ALU.add).then_inc(step, n.inc())
            v.wait_ge(step, n.now())
            v.tensor_tensor(over[:], queued[:].unsqueeze(2).broadcast_to([1, E, t["UMAX"]]), bound_i[:], ALU.is_gt)\
                .then_inc(step, n.inc())
            v.wait_ge(step, n.now())
            v.tensor_reduce(count[:], over[:], AX.X, ALU.add).then_inc(step, n.inc())
            v.memset(begin[:], 0.0).then_inc(step, n.inc())
            v.wait_ge(step, n.now())
            for e in range(E):
                v.scalar_tensor_tensor(out=begin[:, e + 1:e + 2], in0=count[:, e:e + 1], scalar=1.0,
                                       in1=begin[:, e:e + 1], op0=ALU.max, op1=ALU.add).then_inc(step, n.inc())
                v.wait_ge(step, n.now())
            v.tensor_scalar(offset[:], expert[0:1, :], float(QUEUE), None, ALU.mult).then_inc(step, n.inc())
            v.wait_ge(step, n.now())
            v.scalar_tensor_tensor(out=offset[:], in0=begin[:, 0:E], scalar=-float(t["UNIT"]), in1=offset[:],
                                   op0=ALU.mult, op1=ALU.add).then_inc(step, n.inc())
            v.wait_ge(step, n.now())
            v.tensor_copy(first_unit[:], begin[:])
            v.tensor_copy(first_row[:], offset[:])
            v.tensor_copy(first_blank[:], filled[:]).then_inc(step, n.inc())


def run_experts(nc, ctx, t):
    slots, out = t["slots"], t["out"]
    w1, b1, w2, b2 = t["w1"], t["b1"], t["w2"], t["b2"]
    first_unit, first_row, first_blank = t["first_unit"], t["first_row"], t["first_blank"]
    E, D, F = w1.shape
    N = out.shape[0]
    W = slots.shape[1]
    QUEUE, UNIT, UMAX = t["QUEUE"], t["UNIT"], t["UMAX"]
    KD, KF = D // P, F // P
    SUB = UNIT // P
    WF = KD * F
    assert KF * D == WF and E >= 6 and E % 2 == 0
    HUGE = 1e4

    def sb(name, shape, dt):
        return ctx.enter_context(nc.sbuf_tensor(name, shape, dt))

    def sem(name):
        return ctx.enter_context(nc.semaphore(name))

    raw, whi, wlo = t["raw"], t["whi"], t["wlo"]
    b1r = sb("b1r", [E * KF, P], F32)
    b1c = sb("b1c", [P, E * KF], F32)
    b1e = sb("b1e", [P, KF], F32)
    b2b = sb("b2b", [P, E, D], F32)
    b2e = sb("b2e", [P, D], F32)
    pay = sb("u_pay", [P, RING, SUB, W], F32)
    blank = sb("blank", [P, SUB, W], F32)
    scales = sb("scales", [P, SUB, 2], F32)
    token = sb("u_token", [P, SUB], I32)
    hn = sb("hn", [P, SUB, D], F32)
    xhi = sb("xhi", [P, KD, UNIT], F32R)
    xlo = sb("xlo", [P, KD, UNIT], F32R)
    hm = sb("hm", [P, KF, UNIT], F32)
    hhi = sb("hhi", [P, KF, UNIT], F32R)
    hlo = sb("hlo", [P, KF, UNIT], F32R)
    ex = sb("ex", [P, SUB, E], F32)
    total = sb("total", [P, SUB], F32)
    prob = sb("prob", [P, SUB], F32)
    y = sb("y", [P, SUB, D], F32)
    low = sb("low", [P, SUB, D], F32)
    finite = sb("finite", [P, SUB, D], U8)
    yo = sb("yo", [P, SUB, D], F32)
    ident = t["ident"]

    ps_T = ctx.enter_context(nc.psum_tensor("u_T", [P, KD, UNIT], F32))
    ps_H = ctx.enter_context(nc.psum_tensor("u_H", [P, 2, UNIT], F32))
    ps_Y = ctx.enter_context(nc.psum_tensor("u_Y", [P, SUB, 512], F32))

    b1_loaded = sem("b1_loaded")
    b2_loaded = sem("b2_loaded")
    blank_set = sem("blank_set")
    blanked = sem("blanked")
    b1_turned = sem("b1_turned")
    b1_ready = sem("b1_ready")
    b1_own = sem("b1_own")
    b2_own = sem("b2_own")
    raw_loaded = sem("raw_loaded")
    split = sem("split")
    pay_loaded = sem("pay_loaded")
    y_sent = sem("y_sent")
    y_clear = sem("y_clear")
    hn_ready = sem("hn_ready")
    ex_ready = sem("ex_ready")
    prob_ready = sem("prob_ready")
    turned = sem("u_turned")
    xhi_ready = sem("xhi_ready")
    x_ready = sem("x_ready")
    first_done = sem("first_done")
    relu_done = sem("relu_done")
    hhi_ready = sem("hhi_ready")
    hid_ready = sem("hid_ready")
    second_done = sem("second_done")
    y_read = sem("y_read")
    y_ready = sem("y_ready")
    scales_ready = sem("scales_ready")
    step = sem("u_step")
    SEED = dict(y_clear=1, prob_ready=1, relu_done=2, hid_ready=KF, y_read=1, y_ready=RING,
                split=2)

    w1_at = lambda w, b, k, f: w[:, b, k * F + f * P:k * F + (f + 1) * P]
    w2_at = lambda w, b, f: w[:, b, WF + f * D:WF + (f + 1) * D]

    def experts(eng, body):
        def one(e, buf):
            begin = eng.value_load(first_unit[0:1, bass.ds(e, 1)], min_val=0, max_val=(E - 1) * UMAX)
            end = eng.value_load(first_unit[0:1, bass.ds(e + 1, 1)], min_val=1, max_val=E * UMAX)
            body(e, buf, begin, end)
        one(0, 0)
        with eng.Fori(0, (E - 4) // 2) as q:
            one(2 * q + 1, 1)
            one(2 * q + 2, 0)
        for e in range(E - 3, E):
            one(e, e % 2)

    with nc.Block() as block:

        @block.sync
        def _(sp):
            sp.dma_start(b1r[:], b1.rearrange("e (k p) -> (e k) p", p=P)).then_inc(b1_loaded, 16)

            def blank_behind(e):
                row = sp.value_load(first_blank[0:1, bass.ds(e, 1)], min_val=0, max_val=E * QUEUE - UNIT)
                sp.dma_start(slots[bass.ds(row, UNIT), :].rearrange("(s p) w -> p s w", p=P), blank[:])\
                    .then_inc(blanked, 16)
            sp.wait_ge(blank_set, 2)
            blank_behind(0)

            def load(u, row):
                sp.dma_start(pay[:, u % RING, :, :], slots[bass.ds(row, UNIT), :].rearrange("(s p) w -> p s w", p=P))\
                    .then_inc(pay_loaded, 16)

            def expert(e, buf, begin, end):
                sp.wait_ge(blanked, 16 * (e + 1))
                sp.nop(nofuse=True)
                if not (isinstance(e, int) and e == E - 1):
                    blank_behind(e + 1)
                at = sp.value_load(first_row[0:1, bass.ds(e, 1)], min_val=0, max_val=E * QUEUE - UNIT)
                with sp.Fori(begin, end) as u:
                    sp.wait_ge(y_ready, u + (1 - RING + SEED["y_ready"]))
                    sp.nop(nofuse=True)
                    load(u, (u * UNIT + at).with_bounds(min_val=0, max_val=E * QUEUE - UNIT))
                    sp.wait_ge(pay_loaded, 16 * (u + 1))
                    sp.nop(nofuse=True)
            sp.dma_start(b2b[:], b2.partition_broadcast(P)).then_inc(b2_loaded, 16)
            experts(sp, expert)
            units = sp.value_load(first_unit[0:1, E:E + 1], min_val=E, max_val=E * UMAX)
            sp.wait_ge(y_ready, units + (1 - RING + SEED["y_ready"]))
            sp.nop(nofuse=True)
            load(units, 0)
            sp.wait_ge(pay_loaded, 16 * (units + 1))
            sp.nop(nofuse=True)

        @block.gpsimd
        def _(pool):
            def load_weights(e):
                pool.dma_start(raw[:, 0:WF].rearrange("p (k f) -> p k f", k=KD),
                               w1[bass.ds(e, 1)].rearrange("o (k p) f -> (o p) k f", p=P)).then_inc(raw_loaded, 16)
                pool.dma_start(raw[:, WF:2 * WF].rearrange("p (k d) -> p k d", k=KF),
                               w2[bass.ds(e, 1)].rearrange("o (k p) d -> (o p) k d", p=P)).then_inc(raw_loaded, 16)

            def split_weights(e, buf):
                pool.wait_ge(raw_loaded, 32 * e)
                pool.nop(nofuse=True)
                pool.tensor_copy(whi[:, buf, :], raw[:]).then_inc(split, 1)
                pool.wait_ge(split, 2 * e + 1)
                pool.tensor_tensor(wlo[:, buf, :], raw[:], whi[:, buf, :].bitcast(F32), ALU.subtract)\
                    .then_inc(split, 1)

            pool.sem_inc(y_clear, SEED["y_clear"])
            pool.sem_inc(split, SEED["split"])
            pool.wait_ge(pay_loaded, 16)
            pool.nop(nofuse=True)
            load_weights(1)

            def expert(e, buf, begin, end):
                if not (isinstance(e, int) and e == E - 1):
                    split_weights(e + 1, 1 - buf)
                if not (isinstance(e, int) and e >= E - 2):
                    pool.wait_ge(split, 2 * (e + 2))
                    pool.nop(nofuse=True)
                    load_weights(e + 2)
                with pool.Fori(begin, end) as u:
                    pool.wait_ge(y_ready, u + 1 + SEED["y_ready"])
                    pool.nop(nofuse=True)
                    for s in range(SUB):
                        pool.indirect_dma_start(
                            out=out[:, :], out_offset=bass.IndirectOffsetOnAxis(ap=token[:, s:s + 1], axis=0),
                            in_=yo[:, s, :], in_offset=None, bounds_check=N - 1, oob_is_err=False,
                        ).then_inc(y_sent, 16)
                    pool.wait_ge(y_sent, 16 * SUB * (u + 1))
                    pool.nop(nofuse=True)
                    pool.sem_inc(y_clear, 1)
            experts(pool, expert)

        @block.scalar
        def _(act):
            act.sem_inc(relu_done, SEED["relu_done"])

            def upper(u):
                act.wait_ge(turned, u + 1)
                act.activation(xhi[:], ps_T[:], ACT.Copy).then_inc(xhi_ready, 1)

            def expert(e, buf, begin, end):
                act.activation(b1e[:], b1c[:, bass.ds(e * KF, KF)], ACT.Copy).then_inc(b1_own, 1)
                act.wait_ge(b1_own, e + 1)
                act.nop(nofuse=True)
                with act.Fori(begin, end) as u:
                    act.wait_ge(hn_ready, u + 1)
                    act.wait_ge(prob_ready, u + SEED["prob_ready"])
                    act.nop(nofuse=True)
                    act.activation(ex[:], pay[:, u % RING, :, LOGIT:LOGIT + E], ACT.Exp).then_inc(ex_ready, 1)
                    for f in range(KF):
                        act.wait_ge(first_done, KF * u + (f + 1))
                        act.wait_ge(hid_ready, KF * u + (f + 1 - KF + SEED["hid_ready"]))
                        act.activation(hm[:, f, :], ps_H[:, f % 2, :], ACT.Relu, bias=b1e[:, f:f + 1])\
                            .then_inc(relu_done, 1)
                        act.wait_ge(relu_done, KF * u + (f + 1 + SEED["relu_done"]))
                        act.activation(hhi[:, f, :], hm[:, f, :], ACT.Copy).then_inc(hhi_ready, 1)
                    upper(u + 1)
            act.wait_ge(b1_ready, 1)
            upper(0)
            experts(act, expert)

        @block.vector
        def _(v):
            v.memset(blank[:], 0.0).then_inc(blank_set, 1)
            v.wait_ge(blank_set, 1)
            v.memset(blank[:, :, TOKEN:TOKEN + 1].bitcast(I32), 1 << 20).then_inc(blank_set, 1)
            for name, s in (("hid_ready", hid_ready), ("prob_ready", prob_ready), ("y_read", y_read),
                            ("y_ready", y_ready)):
                v.sem_inc(s, SEED[name])
            v.wait_ge(b1_turned, 1)
            v.tensor_copy(b1c[:], ps_T[:, 0, 0:E * KF]).then_inc(b1_ready, 1)
            PER = 6

            def normalise(u):
                v.wait_ge(pay_loaded, 16 * (u + 1))
                v.tensor_copy(scales[:], pay[:, u % RING, :, MEAN:RSTD + 1]).then_inc(scales_ready, 1)
                v.wait_ge(scales_ready, u + 1)
                if not isinstance(u, int):
                    v.wait_ge(turned, u)
                for s in range(SUB):
                    last = v.tensor_scalar(hn[:, s, :], pay[:, u % RING, s, 0:D], scales[:, s, 0:1],
                                           scales[:, s, 1:2], ALU.subtract, ALU.mult)
                last.then_inc(hn_ready, 1)

            def lower(u):
                v.wait_ge(xhi_ready, u + 1)
                v.tensor_tensor(xlo[:], ps_T[:], xhi[:].bitcast(F32), ALU.subtract).then_inc(x_ready, 1)

            def expert(e, buf, begin, end):
                v.tensor_copy(b2e[:], b2b[:, bass.ds(e, 1), :].rearrange("p o d -> p (o d)")).then_inc(b2_own, 1)
                v.wait_ge(b2_own, e + 1)
                v.nop(nofuse=True)
                with v.Fori(begin, end) as u:
                    c = Count(u * PER)
                    normalise(u + 1)
                    for f in range(KF):
                        v.wait_ge(hhi_ready, KF * u + (f + 1))
                        v.tensor_tensor(hlo[:, f, :], hm[:, f, :], hhi[:, f, :].bitcast(F32), ALU.subtract)\
                            .then_inc(hid_ready, 1)
                    v.wait_ge(ex_ready, u + 1)
                    v.tensor_reduce(total[:], ex[:], AX.X, ALU.add).then_inc(step, c.inc())
                    lower(u + 1)
                    v.wait_ge(step, c.now())
                    v.reciprocal(prob[:], total[:]).then_inc(prob_ready, 1)
                    v.wait_ge(second_done, u + 1)
                    for s in range(SUB):
                        last = v.tensor_tensor(y[:, s, :], ps_Y[:, s, 0:D], b2e[:], ALU.add)
                    last.then_inc(y_read, 1)
                    v.wait_ge(prob_ready, u + 1 + SEED["prob_ready"])
                    v.wait_ge(y_read, u + 1 + SEED["y_read"])
                    for s in range(SUB):
                        last = v.tensor_scalar(y[:, s, :], y[:, s, :], prob[:, s:s + 1], None, ALU.mult)
                    last.then_inc(step, c.inc())
                    v.wait_ge(step, c.now())
                    v.tensor_scalar(finite[:], y[:], 0.0, 0.0, ALU.mult, ALU.is_equal)
                    v.tensor_scalar(low[:], y[:], 0.0, -HUGE, ALU.is_lt, ALU.mult).then_inc(step, c.inc())
                    v.wait_ge(y_clear, u + SEED["y_clear"])
                    v.tensor_copy(token[:], pay[:, u % RING, :, TOKEN].bitcast(I32))
                    v.tensor_scalar(yo[:], y[:], 0.0, HUGE, ALU.is_gt, ALU.mult).then_inc(step, c.inc())
                    v.wait_ge(step, c.now())
                    v.tensor_tensor(yo[:], yo[:], low[:], ALU.add).then_inc(step, c.inc())
                    v.wait_ge(step, c.now())
                    v.nop(nofuse=True)
                    v.copy_predicated(yo[:], finite[:], y[:]).then_inc(step, c.inc())
                    v.wait_ge(step, c.now())
                    v.tensor_tensor(yo[:], yo[:], pay[:, u % RING, :, 0:D], ALU.add).then_inc(y_ready, 1)
                    assert c.n == PER, c.n
            normalise(0)
            lower(0)
            v.wait_ge(b2_loaded, 16)
            experts(v, expert)

        @block.tensor
        def _(pe):
            pe.wait_ge(b1_loaded, 16)
            pe.transpose(ps_T[:, 0, 0:E * KF], b1r[:], ident[0:E * KF, 0:E * KF]).then_inc(b1_turned, 1)
            pe.wait_ge(b1_ready, 1)

            def transposes(u):
                pe.wait_ge(hn_ready, u + 1)
                if not isinstance(u, int):
                    pe.wait_ge(x_ready, u)
                for s in range(SUB):
                    for k in range(KD):
                        last = pe.transpose(ps_T[:, k, s * P:(s + 1) * P], hn[:, s, k * P:(k + 1) * P], ident[:])
                last.then_inc(turned, 1)

            transposes(0)

            def expert(e, buf, begin, end):
                pe.wait_ge(split, 2 * (e + 1))
                pe.nop(nofuse=True)
                with pe.Fori(begin, end) as u:
                    pe.wait_ge(x_ready, u + 1)
                    for f in range(KF):
                        pe.wait_ge(relu_done, KF * u + (f - 1 + SEED["relu_done"]))
                        passes = [(w, a, k) for k in range(KD) for w, a in ((whi, xhi), (whi, xlo), (wlo, xhi))]
                        for j, (w, a, k) in enumerate(passes):
                            last = pe.matmul(ps_H[:, f % 2, :], w1_at(w, buf, k, f), a[:, k, :],
                                             start=(j == 0), stop=(j == len(passes) - 1))
                        last.then_inc(first_done, 1)
                    transposes(u + 1)
                    pe.wait_ge(y_read, u + SEED["y_read"])
                    for f in range(KF):
                        pe.wait_ge(hid_ready, KF * u + (f + 1 + SEED["hid_ready"]))
                        for s in range(SUB):
                            cols = slice(s * P, (s + 1) * P)
                            for j, (a, w) in enumerate(((hhi, whi), (hhi, wlo), (hlo, whi))):
                                last = pe.matmul(ps_Y[:, s, 0:D], a[:, f, cols], w2_at(w, buf, f),
                                                 start=(f == 0 and j == 0), stop=(f == KF - 1 and j == 2))
                    last.then_inc(second_done, 1)
            experts(pe, expert)


def build_program(nc, x, src, dst, edge_weight, gate_w, gate_b, w1, b1, w2, b2, out):
    N, D = x.shape
    E = gate_w.shape[1]
    C = max(1, math.ceil(CAPACITY_FACTOR * N / E))
    UNIT = 4 * P
    UMAX = -(-C // UNIT)
    QUEUE = (UMAX + 1) * UNIT
    W = LOGIT + E
    AGG = -(-(N + STEP) // (16 * P)) * (16 * P)
    t = dict(x=x, src=src, dst=dst, weight=edge_weight, gate_w=gate_w, gate_b=gate_b, w1=w1, b1=b1,
             w2=w2, b2=b2, out=out, C=C, QUEUE=QUEUE, UNIT=UNIT, UMAX=UMAX)
    t["agg"] = nc.dram_tensor("agg", (AGG, D), F16, kind="Internal").ap()
    t["slots"] = nc.dram_tensor("slots", (E * QUEUE, W), F32, kind="Internal").ap()
    with ExitStack() as outer:
        t["ident"] = outer.enter_context(nc.sbuf_tensor("ident", [P, P], F32))
        t["before"] = outer.enter_context(nc.sbuf_tensor("before", [P, P], F16))
        t["ones"] = outer.enter_context(nc.sbuf_tensor("ones", [P, P], F16))
        t["eps"] = outer.enter_context(nc.sbuf_tensor("eps", [P, 1], F32))
        for name, n in (("first_unit", E + 1), ("first_row", E), ("first_blank", E)):
            t[name] = outer.enter_context(nc.sbuf_tensor(name, [1, n], I32))
        WF = w1.shape[1] * w1.shape[2] // P
        t["raw"] = outer.enter_context(nc.sbuf_tensor("raw", [P, 2 * WF], F32))
        with ExitStack() as ctx:
            edge_and_constants(nc, ctx, t)
        t["whi"] = outer.enter_context(nc.sbuf_tensor("whi", [P, 2, 2 * WF], F32R))
        t["wlo"] = outer.enter_context(nc.sbuf_tensor("wlo", [P, 2, 2 * WF], F32R))
        for phase in (route_tokens, run_experts):
            with ExitStack() as ctx:
                phase(nc, ctx, t)


_INS = ["x", "src", "dst", "edge_weight", "L0_ffn_gate_w", "L0_ffn_gate_b", "L0_ffn_w1", "L0_ffn_b1",
        "L0_ffn_w2", "L0_ffn_b2"]


def kernel(**inputs):
    import numpy as _np
    import concourse.bacc as _bacc
    from concourse import mybir as _mybir
    from concourse.bass_utils import run_bass_kernel_spmd as _run

    nc = _bacc.Bacc("TRN2", target_bir_lowering=False, num_devices=1)
    arrays, args = {}, []
    for name in _INS:
        a = _np.ascontiguousarray(inputs[name])
        arrays[f"in_{name}"] = a
        args.append(nc.dram_tensor(f"in_{name}", a.shape, _mybir.dt.from_np(a.dtype), kind="ExternalInput").ap())
    out = nc.dram_tensor("out_x", inputs["x"].shape, _mybir.dt.float32, kind="ExternalOutput").ap()
    build_program(nc, *args, out)
    r = _run(nc, [arrays], core_ids=[0])
    return r.results[0]["out_x"]
```
